# Optimizing a Trainium2 kernel written in Bass

```python
import numpy as np
import jax
import jax.numpy as jnp

def _softmax(x, axis=-1):
    return jax.nn.softmax(x, axis=axis)

def _gelu(x):
    return jax.nn.gelu(x, approximate=True)

def _silu(x):
    return jax.nn.silu(x)

def _sigmoid(x):
    return jax.nn.sigmoid(x)

def _layernorm(x, axis=-1, eps=1e-05):
    m = jnp.mean(x, axis=axis, keepdims=True)
    v = jnp.var(x, axis=axis, keepdims=True)
    return (x - m) / jnp.sqrt(v + eps)

def _scatter_add(tgt, idx, src, axis=0):
    return tgt.at[idx].add(src)

def _segment_sum(src, seg, n):
    return jax.ops.segment_sum(src, seg, n)
kernel_name = 'mk_adaln_d1_jaxref_r2_370ba4'

def setup_inputs(seed: int=0):
    np.random.seed(seed)
    _w = jnp.asarray

    def _L0_attn_setup():
        import jax, jax.numpy as jnp
        import numpy as np
        LN_EPS = 1e-05

        def _layernorm(x, gamma, beta):
            mu = jnp.mean(x, axis=-1, keepdims=True)
            var = jnp.var(x, axis=-1, keepdims=True)
            return (x - mu) * jax.lax.rsqrt(var + LN_EPS) * gamma + beta
        key = jax.random.key(seed)
        ks = jax.random.split(key, 6)
        B, T, C = (4, 2048, 512)
        xavier = float(np.sqrt(6.0 / (C + C)))
        inp = {'x': jax.random.normal(ks[0], (B, T, C), dtype=jnp.float32), 'time_decay': jnp.zeros((C,), dtype=jnp.float32), 'time_first': jnp.ones((C,), dtype=jnp.float32), 'Wk': jax.random.uniform(ks[1], (C, C), jnp.float32, -xavier, xavier), 'Wv': jax.random.uniform(ks[2], (C, C), jnp.float32, -xavier, xavier), 'Wr': jax.random.uniform(ks[3], (C, C), jnp.float32, -xavier, xavier), 'Wo': jax.random.uniform(ks[4], (C, C), jnp.float32, -xavier, xavier), 'ln_gamma': jnp.ones((C,), dtype=jnp.float32), 'ln_beta': jnp.zeros((C,), dtype=jnp.float32)}
        return inp
    _L0_attn_in = _L0_attn_setup()

    def _L0_ffn_setup():
        import jax, jax.numpy as jnp
        from jax import lax
        import numpy as np
        D_MODEL = 512
        HIDDEN = 256
        N_EXPERTS = 32
        TOP_K = 2
        B, S = (1, 2048)

        def _moe_group(x2, router_w, wg, wu, wd, top_k):
            T = x2.shape[0]
            n_experts = router_w.shape[1]
            logits = x2 @ router_w
            scores = jax.nn.softmax(logits, axis=-1)
            expert_weights, expert_indices = lax.top_k(scores, top_k)
            flat_e = expert_indices.reshape(-1)
            flat_w = expert_weights.reshape(-1)
            flat_t = jnp.repeat(jnp.arange(T), top_k)
            order = jnp.argsort(flat_e)
            tok = flat_t[order]
            xs = x2[tok]
            group_sizes = jnp.bincount(flat_e, length=n_experts).astype(jnp.int32)
            gate = lax.ragged_dot(xs, wg, group_sizes)
            up = lax.ragged_dot(xs, wu, group_sizes)
            ys = lax.ragged_dot(jax.nn.silu(gate) * up, wd, group_sizes)
            ys = ys * flat_w[order][:, None]
            return jnp.zeros_like(x2).at[tok].add(ys)
        key = jax.random.key(seed)
        ks = jax.random.split(key, 9)
        w = lambda k, shape: jax.random.normal(k, shape, dtype=jnp.float32) * 0.02
        return {'x': jax.random.normal(ks[0], (B, S, D_MODEL), dtype=jnp.float32), 'router_w0': w(ks[1], (D_MODEL, N_EXPERTS)), 'wg0': w(ks[2], (N_EXPERTS, D_MODEL, HIDDEN)), 'wu0': w(ks[3], (N_EXPERTS, D_MODEL, HIDDEN)), 'wd0': w(ks[4], (N_EXPERTS, HIDDEN, D_MODEL)), 'router_w1': w(ks[5], (D_MODEL, N_EXPERTS)), 'wg1': w(ks[6], (N_EXPERTS, D_MODEL, HIDDEN)), 'wu1': w(ks[7], (N_EXPERTS, D_MODEL, HIDDEN)), 'wd1': w(ks[8], (N_EXPERTS, HIDDEN, D_MODEL))}
    _L0_ffn_in = _L0_ffn_setup()
    _L0_c = _w((lambda *s: np.random.randn(*s).astype(np.float32) * 0.05)(8, 512))
    _L0_wmod = _w((lambda *s: np.random.randn(*s).astype(np.float32) * 0.05)(512, 6 * 512) * 512 ** (-0.5))
    _d = {'L0_attn_x': _L0_attn_in['x'], 'L0_attn_time_decay': _L0_attn_in['time_decay'], 'L0_attn_time_first': _L0_attn_in['time_first'], 'L0_attn_Wk': _L0_attn_in['Wk'], 'L0_attn_Wv': _L0_attn_in['Wv'], 'L0_attn_Wr': _L0_attn_in['Wr'], 'L0_attn_Wo': _L0_attn_in['Wo'], 'L0_attn_ln_gamma': _L0_attn_in['ln_gamma'], 'L0_attn_ln_beta': _L0_attn_in['ln_beta'], 'L0_ffn_router_w0': _L0_ffn_in['router_w0'], 'L0_ffn_wg0': _L0_ffn_in['wg0'], 'L0_ffn_wu0': _L0_ffn_in['wu0'], 'L0_ffn_wd0': _L0_ffn_in['wd0'], 'L0_ffn_router_w1': _L0_ffn_in['router_w1'], 'L0_ffn_wg1': _L0_ffn_in['wg1'], 'L0_ffn_wu1': _L0_ffn_in['wu1'], 'L0_ffn_wd1': _L0_ffn_in['wd1'], 'L0_c': _L0_c, 'L0_wmod': _L0_wmod}
    _x0 = _d['L0_attn_x']
    _d['L0_attn_x'] = jax.random.normal(jax.random.fold_in(jax.random.key(seed), 1), (8, 2048, 512), dtype=_x0.dtype)
    del _x0
    return _d

def reference(L0_attn_x, L0_attn_time_decay, L0_attn_time_first, L0_attn_Wk, L0_attn_Wv, L0_attn_Wr, L0_attn_Wo, L0_attn_ln_gamma, L0_attn_ln_beta, L0_ffn_router_w0, L0_ffn_wg0, L0_ffn_wu0, L0_ffn_wd0, L0_ffn_router_w1, L0_ffn_wg1, L0_ffn_wu1, L0_ffn_wd1, L0_c, L0_wmod):

    def _L0_attn_ref(x, time_decay, time_first, Wk, Wv, Wr, Wo, ln_gamma, ln_beta):
        import jax, jax.numpy as jnp
        import numpy as np
        LN_EPS = 1e-05

        def _layernorm(x, gamma, beta):
            mu = jnp.mean(x, axis=-1, keepdims=True)
            var = jnp.var(x, axis=-1, keepdims=True)
            return (x - mu) * jax.lax.rsqrt(var + LN_EPS) * gamma + beta
        B, T, C = x.shape
        xn = _layernorm(x, ln_gamma, ln_beta)
        k = jnp.einsum('btc,dc->btd', xn, Wk)
        v = jnp.einsum('btc,dc->btd', xn, Wv)
        r = jnp.einsum('btc,dc->btd', xn, Wr)
        td = jax.nn.sigmoid(time_decay)
        tf = jax.nn.sigmoid(time_first)
        kv = k * v
        t_idx = jnp.arange(T, dtype=x.dtype)[None, :, None]
        weighted_kv = kv * jnp.power(td[None, None, :], t_idx)
        csum = jnp.cumsum(weighted_kv, axis=1)
        shifted = jnp.concatenate([jnp.zeros((B, 1, C), dtype=x.dtype), csum[:, :-1]], axis=1)
        wkv = tf * kv + td * shifted
        out = jnp.einsum('btc,dc->btd', jax.nn.sigmoid(r) * wkv, Wo)
        return out

    def _L0_ffn_ref(x, router_w0, wg0, wu0, wd0, router_w1, wg1, wu1, wd1):
        import jax, jax.numpy as jnp
        from jax import lax
        import numpy as np
        D_MODEL = 512
        HIDDEN = 256
        N_EXPERTS = 32
        TOP_K = 2
        B, S = (1, 2048)

        def _moe_group(x2, router_w, wg, wu, wd, top_k):
            T = x2.shape[0]
            n_experts = router_w.shape[1]
            logits = x2 @ router_w
            scores = jax.nn.softmax(logits, axis=-1)
            expert_weights, expert_indices = lax.top_k(scores, top_k)
            flat_e = expert_indices.reshape(-1)
            flat_w = expert_weights.reshape(-1)
            flat_t = jnp.repeat(jnp.arange(T), top_k)
            order = jnp.argsort(flat_e)
            tok = flat_t[order]
            xs = x2[tok]
            group_sizes = jnp.bincount(flat_e, length=n_experts).astype(jnp.int32)
            gate = lax.ragged_dot(xs, wg, group_sizes)
            up = lax.ragged_dot(xs, wu, group_sizes)
            ys = lax.ragged_dot(jax.nn.silu(gate) * up, wd, group_sizes)
            ys = ys * flat_w[order][:, None]
            return jnp.zeros_like(x2).at[tok].add(ys)
        b, s, d = x.shape
        x2 = x.reshape(-1, d)
        out0 = _moe_group(x2, router_w0, wg0, wu0, wd0, TOP_K)
        out1 = _moe_group(x2, router_w1, wg1, wu1, wd1, TOP_K)
        out = (out0 * TOP_K + out1 * TOP_K) / (TOP_K + TOP_K)
        return out.reshape(b, s, d)
    x = L0_attn_x
    mod = (_silu(L0_c) @ L0_wmod).reshape(L0_c.shape[0], 6, 1, -1)
    sa, ca, ga, sb, cb, gb = (mod[:, 0], mod[:, 1], mod[:, 2], mod[:, 3], mod[:, 4], mod[:, 5])
    ga = (2 * (ga >= 0) - 1) * jnp.maximum(jnp.abs(ga), 0.25)
    gb = (2 * (gb >= 0) - 1) * jnp.maximum(jnp.abs(gb), 0.25)
    h = _layernorm(x, axis=-1) * (1 + ca) + sa
    x = x + ga * _L0_attn_ref(h, L0_attn_time_decay, L0_attn_time_first, L0_attn_Wk, L0_attn_Wv, L0_attn_Wr, L0_attn_Wo, L0_attn_ln_gamma, L0_attn_ln_beta)
    h = _layernorm(x, axis=-1) * (1 + cb) + sb
    x = x + gb * _L0_ffn_ref(h, L0_ffn_router_w0, L0_ffn_wg0, L0_ffn_wu0, L0_ffn_wd0, L0_ffn_router_w1, L0_ffn_wg1, L0_ffn_wu1, L0_ffn_wd1)
    return x

_drawn_inputs = setup_inputs


def setup_inputs(seed=0):
    import zlib

    import numpy as np

    out = dict(_drawn_inputs(seed))
    spreads = {'L0_attn_time_decay': (0.0, 0.8),
     'L0_attn_time_first': (1.0, 0.6),
     'L0_attn_ln_gamma': (1.0, 0.2),
     'L0_attn_ln_beta': (0.0, 0.428)}
    factors = {'L0_ffn_router_w0': 8.0,
     'L0_ffn_wg0': 8.0,
     'L0_ffn_wu0': 8.0,
     'L0_ffn_wd0': 8.0,
     'L0_ffn_router_w1': 8.0,
     'L0_ffn_wg1': 8.0,
     'L0_ffn_wu1': 8.0,
     'L0_ffn_wd1': 8.0}
    for name, (base, spread) in spreads.items():
        noise = np.random.default_rng([zlib.crc32(name.encode()), seed]).standard_normal(out[name].shape)
        drawn = base * np.exp(spread * noise) if base else spread * noise
        out[name] = jnp.asarray(drawn.astype(out[name].dtype))
    for name, factor in factors.items():
        out[name] = (out[name] * factor).astype(out[name].dtype)
    return out
```

```python
from contextlib import ExitStack

import concourse.bass as bass
import concourse.mybir as mybir

P = 128
F32 = mybir.dt.float32
F32R = mybir.dt.float32r
BF16 = mybir.dt.bfloat16
U32 = mybir.dt.uint32
ALU = mybir.AluOpType
ACT = mybir.ActivationFunctionType
AX_X = mybir.AxisListType.X

EPS = 1e-5
TT = 512
TJ = TT // P
PAGE = 256
BANK = 512
NBANK = 8

CA1, SA, CB1, SB, GA, GBH = range(6)

PROJ, OUTP, RANK, FRONTT, BACKT, LOGIT = (0, 8, 11, 14), 3, 7, 17, 21, 25
GROUPS = 26


def wait(eng, sem, value):
    if isinstance(value, int) and value <= 0:
        return
    eng.wait_ge(sem, value)


def gate(eng, *waits):
    waits = [(sem, value if isinstance(value, int) else eng.to_reg(value)) for sem, value in waits]
    if not isinstance(waits[0][1], int):
        eng.wait_ge(waits[0][0], 1)
    for sem, value in waits:
        wait(eng, sem, value)


def cnt(b, s, per, k):
    if isinstance(b, int):
        return (4 * b + s) * per + k
    return b * (4 * per) + (s * per + k)


def dcnt(b, s, k=1):
    q = 16 * k
    if isinstance(b, int):
        return (2 * b + s // 2 + 1) * q
    return b * (2 * q) + (s // 2 + 1) * q


def build(nc, x, vec, wkvr, wo, rw, wex, cT, wmod, out):
    B, T, C = x.shape
    N = B * T
    KC = C // P
    STEPS = N // TT
    SPB = T // TT
    G, E = 2, rw.shape[1] // 2
    GE = G * E
    H = 256
    WROW = KC * 2 * H + (H // P) * C
    NPG = 2 * N // PAGE + E
    NPG += NPG % 2
    FILL = 8
    NPAGES = FILL * (6 + 2 * B)
    assert SPB == 4 and KC == 4 and C == BANK and NPG <= 2 * P and NPG < NPAGES
    assert GROUPS * SPB % NBANK == 0

    xf = x.rearrange("b t c -> (b t) c")
    outf = out.rearrange("b t c -> (b t) c")
    x1_d = nc.dram_tensor("x1_d", (N, C), F32, kind="Internal").ap()
    lg_d = nc.dram_tensor("lg_d", (P, STEPS * (4 * GE + 16)), F32, kind="Internal").ap()
    slots_d = nc.dram_tensor("slots_d", (P, STEPS * 16), U32, kind="Internal").ap()
    hist_d = nc.dram_tensor("hist_d", (STEPS, 2 * GE), F32, kind="Internal").ap()
    mod_d = nc.dram_tensor("mod_d", (B, 6 * C), F32, kind="Internal").ap()
    own_d = nc.dram_tensor("own_d", (G * 2, P), U32, kind="Internal").ap()
    pages = [nc.dram_tensor(f"pages{g}_d", (NPAGES * PAGE, C), F32, kind="Internal").ap()
             for g in range(G)]

    with ExitStack() as whole:
        ident = whole.enter_context(nc.sbuf_tensor("ident", [P, P], F32))
        ps = whole.enter_context(nc.psum_tensor("ps", [P, NBANK, BANK], F32))

        with nc.cleanup_on_exit():
            stage_a(nc, locals())
        wts = whole.enter_context(nc.sbuf_tensor("wts", [P, STEPS * 16], F32))
        stage_b(nc, locals())
        for g in range(G):
            stage_c(nc, g, locals())
        stage_d(nc, locals())


def stage_a(nc, L):
    B, KC, GE, E, G, C = L["B"], L["KC"], L["GE"], L["E"], L["G"], L["C"]
    N, FILL = L["N"], L["FILL"]
    ps, ident = L["ps"], L["ident"]
    slots_d = L["slots_d"]
    xf, x1_d, lg_d, hist_d, mod_d, pages = L["xf"], L["x1_d"], L["lg_d"], L["hist_d"], L["mod_d"], L["pages"]
    R = TJ * G

    with ExitStack() as ctx:
        def sb(name, shape, dt=F32):
            return ctx.enter_context(nc.sbuf_tensor(name, shape, dt))

        def sem(name):
            return nc.alloc_semaphore(name)

        xin = sb("xin", [P, 4, TJ, C])
        hb = sb("hb", [P, TJ, C])
        h2T = hb
        xTh = sb("xTh", [P, KC, TT], F32R)
        xTl = sb("xTl", [P, KC, TT], F32R)
        wTh = sb("wTh", [P, 3, KC, C], F32R)
        wTl = sb("wTl", [P, 3, KC, C], F32R)
        woh = sb("woh", [P, KC, C], F32R)
        wol = sb("wol", [P, KC, C], F32R)
        pw = sb("pw", [P, KC, TT])
        gs = sb("gs", [P, KC, 4])
        cs = sb("cs", [P, KC, TT + 1])
        kb = sb("kb", [P, TT])
        sg = sb("sg", [P, 2, TT])
        kv = sb("kv", [P, TT])
        wk = sb("wk", [P, TT])
        aa = sb("aa", [P, 2, TT])
        sTh = sb("sTh", [P, KC, TT], F32R)
        sTl = sb("sTl", [P, KC, TT], F32R)
        h2 = sb("h2", [P, 2, TJ, C])
        wo_s = h2[:, 1]
        rws = sb("rws", [P, KC, GE])
        lgt = sb("lgt", [P, R * E + 2 * R])
        lg = lgt[:, 0:R * E].rearrange("p (r e) -> p r e", r=R)
        m8 = sb("m8", [P, R, 8])
        i8 = sb("i8", [P, R, 8], U32)
        ixf = sb("ixf", [P, R, 2])
        hit1 = sb("hit1", [P, R, E])
        hit2 = sb("hit2", [P, R, E])
        hits = sb("hits", [P, TJ, GE], BF16)
        qq = sb("qq", [P, TJ, GE])
        ee = sb("ee", [P, TJ, GE])
        tot = sb("tot", [P, GE])
        two = sb("two", [P, GE])
        alloc = sb("alloc", [P, 2, GE])
        incl = sb("incl", [P, GE])
        dpg = sb("dpg", [P, GE])
        used = sb("used", [P, GE])
        cur = sb("cur", [P, GE])
        fre = sb("fre", [P, G])
        slf = sb("slf", [P, 2, R])
        sidx = sb("sidx", [P, 2, TJ * G * 2], U32)
        mod = sb("mod", [P, 5, C])
        zrow = sb("zrow", [P, 1, C])
        iota = sb("iota", [P, E])
        ones = sb("ones", [P, 1])
        tri = sb("tri", [P, P], BF16)
        oneb = sb("oneb", [P, P], BF16)
        bias = sb("bias", [P, 3, KC])
        tdc = sb("tdc", [P, KC])
        tfc = sb("tfc", [P, KC])
        gmc = sb("gmc", [P, KC])
        btc = sb("btc", [P, KC])
        half = sb("half", [P, TJ])
        stf, mvf, vaf, rsf = sb("stf", [P, TJ, 6]), sb("mvf", [P, TJ, 2]), sb("vaf", [P, TJ]), sb("rsf", [P, TJ])
        nmg = sb("nmg", [P, TJ])
        stg, mvg, vag, rsg = sb("stg", [P, TJ, 6]), sb("mvg", [P, TJ, 2]), sb("vag", [P, TJ]), sb("rsg", [P, TJ])
        stb, mvb, vab, rsb = sb("stb", [P, TJ, 6]), sb("mvb", [P, TJ, 2]), sb("vab", [P, TJ]), sb("rsb", [P, TJ])

        setup(nc, L, locals())

        x_in = [sem(f"x_in{i}") for i in range(4)]
        x1_out = sem("x1_out")
        lg_out, hist_out = sem("lg_out"), sem("hist_out")
        slots_out = [sem("slots_out0"), sem("slots_out1")]
        modf_in, modb_in, ga_in, wo_in = sem("modf_in"), sem("modb_in"), sem("ga_in"), sem("wo_in")
        cleared = [sem("cleared0"), sem("cleared1")]
        scattered = [sem("scattered0"), sem("scattered1")]
        proj_done = sem("proj_done")
        backT_done = sem("backT_done")
        logit_done = sem("logit_done")
        frontT_done = sem("frontT_done")
        out_done = sem("out_done")
        rank_done = sem("rank_done")
        k_biased = sem("k_biased")
        r_sig = sem("r_sig")
        tfkv = sem("tfkv")
        s_hi = sem("s_hi")
        h2T_copied = sem("h2T_copied")
        lg_copied = sem("lg_copied")
        x_hi = sem("x_hi")
        wo_hi = sem("wo_hi")
        z_ready = sem("z_ready")
        s_ready, s_split = sem("s_ready"), sem("s_split")
        f_rstd, g_rstd, b_rstd = sem("f_rstd"), sem("g_rstd"), sem("b_rstd")
        f_stats, f_aggr, f_var = sem("f_stats"), sem("f_aggr"), sem("f_var")
        h_half, h_ready = sem("h_half"), sem("h_ready")
        g_stats, g_aggr, g_var = sem("g_stats"), sem("g_aggr"), sem("g_var")
        g_nm = sem("g_nm")
        x_split = sem("x_split")
        kv_ready, carry, wk_ready, scan = sem("kv_ready"), sem("carry"), sem("wk_ready"), sem("scan")
        wkv_ready = sem("wkv_ready")
        x1_ready = sem("x1_ready")
        b_stats, b_aggr, b_var = sem("b_stats"), sem("b_aggr"), sem("b_var")
        h2_half, h2_ready = sem("h2_half"), sem("h2_ready")
        top_max, top_idx = sem("top_max"), sem("top_idx")
        top_kept, idx_f, hit, hits_ready = sem("top_kept"), sem("idx_f"), sem("hit"), sem("hits_ready")
        rank_read, page_op, slot_ready = sem("rank_read"), sem("page_op"), sem("slot_ready")
        wo_scaled, wo_split = sem("wo_scaled"), sem("wo_split")
        PGOPS = 17

        def bank(s, q):
            return ps[:, (s * GROUPS + q) % NBANK, :]

        def worked(n, q):
            if n < 0:
                return n == -1 and FRONTT <= q < BACKT
            behind = 2 if q == RANK else 1 if OUTP <= q < RANK or q >= BACKT else 0
            return n - behind >= 0 and n - behind < 4 * B

        def bank_free(pe, b, s, q):
            at = s * GROUPS + q - NBANK
            while isinstance(b, int) and at > -GROUPS and not worked(4 * b + at // GROUPS, at % GROUPS):
                at -= NBANK
            s0, q0 = at // GROUPS, at % GROUPS
            if q0 == LOGIT:
                who, m, v, s0 = lg_copied, 1, 1, s0 - 1
            elif q0 >= BACKT:
                who, m, v, s0 = h2T_copied, 4, q0 - BACKT + 1, s0 - 1
            elif q0 >= FRONTT:
                who, m, v, s0 = x_split, 4, q0 - FRONTT + 1, s0 + 1
            elif q0 == RANK:
                who, m, v, s0 = rank_read, 2, 2, s0 - 2
            elif OUTP <= q0 < RANK:
                who, m, v, s0 = x1_ready, 4, q0 - OUTP + 1, s0 - 1
            else:
                dc = max(i for i in range(KC) if PROJ[i] <= q0)
                who, m, v = (k_biased, kv_ready, r_sig)[q0 - PROJ[dc]], 4, dc + 1
            wait(pe, who, cnt(b, s0, m, v))

        block = ctx.enter_context(nc.Block())

        @block.sync
        def _(sp):
            def load_x(b, s):
                row = (b * (4 * TT) + s * TT) if s < 4 else ((b + 1) % B) * (4 * TT) + (s - 4) * TT
                gate(sp, (x1_out, cnt(b, s - 4, 16, 16)), (h2_half, cnt(b, s - 4, 4, 4)))
                sp.dma_start(xin[:, s % 4], xf[bass.ds(row, TT), :].rearrange("(j p) c -> p j c", p=P)
                             ).then_inc(x_in[s % 4], 16)

            def store_x1(b, s):
                wait(sp, x1_ready, cnt(b, s, 4, 4))
                row = b * (4 * TT) + s * TT
                sp.dma_start(x1_d[bass.ds(row, TT), :].rearrange("(j p) c -> p j c", p=P), xin[:, s % 4]
                             ).then_inc(x1_out, 16)

            def store_logits(b, s):
                gate(sp, (top_kept, cnt(b, s, 1, 1)))
                n = R * E + 2 * R
                sp.dma_start(lg_d[:, bass.ds(b * (4 * n) + s * n, n)], lgt[:]).then_inc(lg_out, 16)

            def store_pages(b, s):
                wait(sp, page_op, cnt(b, s, PGOPS, PGOPS))
                row = b * 4 + s
                sp.dma_start(hist_d[bass.ds(row, 1), :], alloc[0:1].rearrange("p a e -> p (a e)")
                             ).then_inc(hist_out, 16)
                gate(sp, (slot_ready, cnt(b, s, 2, 2)))
                sp.dma_start(slots_d[:, bass.ds(b * 64 + s * 16, 16)], sidx[:, s % 2, :]).then_inc(slots_out[s % 2], 16)

            def load_mod(b, first, n, sem_):
                sp.dma_start(mod[:, first:first + n, :].rearrange("p r c -> p (r c)"),
                             mod_d[bass.ds(b, 1), first * C:(first + n) * C].to_broadcast([P, n * C])
                             ).then_inc(sem_, 16)

            zero = zrow[:]

            def fill(g, first, n):
                dst = pages[g][bass.ds(first * PAGE, n * PAGE), :].rearrange("(p r) c -> p r c", p=P)
                sp.dma_start(dst, zero.to_broadcast([P, n * PAGE // P, C])).then_inc(cleared[g], 16)

            def load_wo():
                sp.dma_start(wo_s, L["wo"].rearrange("(k p) d -> p k d", p=P)).then_inc(wo_in, 16)

            def step(b, s, first):
                if s == 0 and not first:
                    load_mod(b, GA, 1, ga_in)
                    wait(sp, scattered[1], dcnt(b, -3, 16))
                    wait(sp, backT_done, cnt(b, -3, 4, 4))
                    load_wo()
                load_x(b, s + 2)
                if not (first and s < 2):
                    store_logits(b, s - 2)
                if s == 2:
                    wait(sp, h_ready, cnt(b, 3, 4, 4))
                    load_mod((b + 1) % B, CA1, 2, modf_in)
                if not (first and s == 0):
                    store_x1(b, s - 1)
                if not (first and s < 2):
                    store_pages(b, s - 2)
                if s == 0 and not first:
                    wait(sp, h2_ready, cnt(b, -1, 4, 4))
                    load_mod(b, CB1, 2, modb_in)
                if first and s < 2:
                    for k in ((0, 1, 2), (3, 4, 5, 6))[s]:
                        for g in range(G):
                            wait(sp, cleared[g], 16 * k)
                            fill(g, k * FILL, FILL)
                elif s % 2 == 0:
                    for g in range(G):
                        k = 6 + (b * 2 + s // 2)
                        wait(sp, cleared[g], (k * 16) if isinstance(k, int) else b * 32 + (6 + s // 2) * 16)
                        fill(g, k * FILL, FILL)

            load_x(0, 0)
            load_mod(0, CA1, 2, modf_in)
            load_x(0, 1)
            load_mod(0, CB1, 2, modb_in)
            load_mod(0, GA, 1, ga_in)
            load_wo()
            for s in range(4):
                step(0, s, True)
            with sp.Fori(1, B) as b:
                for s in range(4):
                    step(b, s, False)
            store_logits(B, -2)
            store_x1(B, -1)
            store_pages(B, -2)
            store_logits(B, -1)
            store_pages(B, -1)
            sp.wait_ge(x1_out, 16 * 4 * B)
            for par in range(2):
                sp.wait_ge(slots_out[par], 16 * 2 * B)
                sp.wait_ge(x_in[par], 16 * (B + 1))
                sp.wait_ge(x_in[2 + par], 16 * B)
                sp.wait_ge(cleared[par], 16 * (6 + 2 * B))
            sp.wait_ge(lg_out, 16 * 4 * B)
            sp.wait_ge(hist_out, 16 * 4 * B)
            sp.wait_ge(modf_in, 16 * (B + 1))

        @block.tensor
        def _(pe):
            def split3(o, lh, ll, rh, rl, first, last):
                nc.tensor.matmul(o, lh, rh, start=first, stop=False)
                nc.tensor.matmul(o, lh, rl, start=False, stop=False)
                return nc.tensor.matmul(o, ll, rh, start=False, stop=last)

            def project(b, s, dc):
                d = slice(dc * P, (dc + 1) * P)
                for w in range(3):
                    q = PROJ[dc] + w
                    bank_free(pe, b, s, q)
                    for k in range(KC):
                        if dc == 0 and w == 0:
                            pe.wait_ge(x_split, cnt(b, s, 4, k + 1))
                        last = split3(bank(s, q), wTh[:, w, k, d], wTl[:, w, k, d],
                                      xTh[:, k, :], xTl[:, k, :], k == 0, k == KC - 1)
                    last.then_inc(proj_done, 1)

            def back(b, s):
                pe.wait_ge(h2_ready, cnt(b, s - 1, 4, 4))
                for k in range(KC):
                    bank_free(pe, b, s, BACKT + k)
                    for j in range(TJ):
                        last = nc.tensor.transpose(bank(s, BACKT + k)[:, j * P:(j + 1) * P],
                                                   h2[:, (s - 1) % 2, j, k * P:(k + 1) * P], ident[:])
                    last.then_inc(backT_done, 1)
                bank_free(pe, b, s, LOGIT)
                pe.wait_ge(h2T_copied, cnt(b, s - 1, 4, 4))
                for j in range(TJ):
                    for k in range(KC):
                        last = nc.tensor.matmul(bank(s, LOGIT)[:, j * GE:(j + 1) * GE],
                                                h2T[:, k, j * P:(j + 1) * P], rws[:, k, :],
                                                start=(k == 0), stop=(k == KC - 1))
                last.then_inc(logit_done, 1)

            def front(b, s):
                pe.wait_ge(z_ready, cnt(b, s + 1, 4, 4))
                for k in range(KC):
                    bank_free(pe, b, s, FRONTT + k)
                    for j in range(TJ):
                        last = nc.tensor.transpose(bank(s, FRONTT + k)[:, j * P:(j + 1) * P],
                                                   hb[:, j, k * P:(k + 1) * P], ident[:])
                    last.then_inc(frontT_done, 1)

            def output(b, s):
                pe.wait_ge(s_split, cnt(b, s - 1, 4, 4))
                if s == 1:
                    pe.wait_ge(wo_split, b + 1)
                for j in range(TJ):
                    t = slice(j * P, (j + 1) * P)
                    bank_free(pe, b, s, OUTP + j)
                    for k in range(KC):
                        last = split3(bank(s, OUTP + j), sTh[:, k, t], sTl[:, k, t],
                                      woh[:, k, :], wol[:, k, :], k == 0, k == KC - 1)
                    last.then_inc(out_done, 1)

            def ranks(b, s):
                bank_free(pe, b, s, RANK)
                pe.wait_ge(hits_ready, cnt(b, s - 2, 1, 1))
                o = bank(s, RANK)
                for j in range(TJ):
                    for i in range(j):
                        nc.tensor.matmul(o[:, j * GE:(j + 1) * GE], oneb[:], hits[:, i, :], start=(i == 0), stop=False)
                    nc.tensor.matmul(o[:, j * GE:(j + 1) * GE], tri[:], hits[:, j, :], start=(j == 0), stop=True)
                for j in range(TJ):
                    last = nc.tensor.matmul(o[:, TJ * GE:(TJ + 1) * GE], oneb[:], hits[:, j, :],
                                            start=(j == 0), stop=(j == TJ - 1))
                last.then_inc(rank_done, 1)

            def step(b, s, first):
                project(b, s, 0)
                if not (first and s == 0):
                    output(b, s)
                if not (first and s < 2):
                    ranks(b, s)
                for dc in range(1, KC):
                    project(b, s, dc)
                front(b, s)
                if not (first and s == 0):
                    back(b, s)

            front(0, -1)
            for s in range(4):
                step(0, s, True)
            with pe.Fori(1, B) as b:
                for s in range(4):
                    step(b, s, False)
            output(B, 0)
            ranks(B, 0)
            back(B, 0)
            ranks(B, 1)

        @block.scalar
        def _(act):
            def chunk_kr(b, s, dc):
                act.wait_ge(proj_done, cnt(b, s, 12, 3 * dc + 1))
                wait(act, kv_ready, cnt(b, s, 4, dc))
                nc.scalar.activation(kb[:], bank(s, PROJ[dc]), ACT.Identity,
                                     bias=bias[:, 0, dc:dc + 1]).then_inc(k_biased, 1)
                act.wait_ge(proj_done, cnt(b, s, 12, 3 * dc + 3))
                wait(act, s_split, cnt(b, s, 4, dc - 1))
                nc.scalar.activation(sg[:, dc % 2, :], bank(s, PROJ[dc] + 2), ACT.Sigmoid,
                                     bias=bias[:, 2, dc:dc + 1]).then_inc(r_sig, 1)

            def chunk_v(b, s, dc):
                act.wait_ge(kv_ready, cnt(b, s, 4, dc + 1))
                wait(act, s_ready, cnt(b, s, 4, dc - 1))
                nc.scalar.activation(aa[:, dc % 2, :], kv[:], ACT.Copy,
                                     scale=tfc[:, dc:dc + 1]).then_inc(tfkv, 1)

            def hi(b, s, dc):
                act.wait_ge(s_ready, cnt(b, s, 4, dc + 1))
                wait(act, out_done, cnt(b, s - 1, 4, 4))
                nc.scalar.copy(sTh[:, dc, :], sg[:, dc % 2, :]).then_inc(s_hi, 1)

            def wo(b):
                act.wait_ge(wo_scaled, b + 1)
                wait(act, out_done, cnt(b, -1, 4, 4))
                nc.scalar.copy(woh[:], wo_s).then_inc(wo_hi, 1)

            def turned(b, s):
                for k in range(KC):
                    act.wait_ge(backT_done, cnt(b, s - 1, 4, k + 1))
                    nc.scalar.copy(h2T[:, k, :], bank(s, BACKT + k)).then_inc(h2T_copied, 1)

            def logits(b, s):
                act.wait_ge(logit_done, cnt(b, s - 1, 1, 1))
                wait(act, lg_out, cnt(b, s - 2, 16, 16))
                wait(act, top_idx, cnt(b, s - 2, 8, 8))
                nc.scalar.copy(lgt[:, 0:R * E], bank(s, LOGIT)[:, 0:R * E]).then_inc(lg_copied, 1)

            def normed(b, s):
                act.wait_ge(g_nm, cnt(b, s + 1, 1, 1))
                for j in range(TJ):
                    nc.scalar.activation(hb[:, j, :], hb[:, j, :], ACT.Identity,
                                         bias=nmg[:, j:j + 1], scale=rsg[:, j:j + 1]).then_inc(z_ready, 1)

            def front(b, s):
                for k in range(KC):
                    act.wait_ge(frontT_done, cnt(b, s + 1, 4, k + 1))
                    wait(act, proj_done, cnt(b, s, 12, 12))
                    nc.scalar.copy(xTh[:, k, :], bank(s, FRONTT + k)).then_inc(x_hi, 1)

            def step(b, s, first):
                for dc in range(3):
                    chunk_kr(b, s, dc)
                    chunk_v(b, s, dc)
                    hi(b, s, dc)
                    if dc == 0:
                        normed(b, s)
                        if s == 0:
                            wo(b)
                chunk_kr(b, s, 3)
                chunk_v(b, s, 3)
                front(b, s)
                if not (first and s == 0):
                    turned(b, s)
                hi(b, s, 3)
                if not (first and s == 0):
                    logits(b, s)

            normed(0, -1)
            front(0, -1)
            for s in range(4):
                step(0, s, True)
            with act.Fori(1, B) as b:
                for s in range(4):
                    step(b, s, False)
            turned(B, 0)
            logits(B, 0)

        @block.gpsimd
        def _(pool):
            def rstd(var_sem, var, per_done, rs, done, b, s):
                pool.wait_ge(var_sem, cnt(b, s, 1, 1))
                wait(pool, per_done, cnt(b, s - 1, 4, 4))
                nc.gpsimd.tensor_tensor(rs[:], var[:], half[:], ALU.pow).then_inc(done, 1)

            def receive(b, s, dc):
                pool.wait_ge(wkv_ready, cnt(b, s, 4, dc + 1))
                pool.wait_ge(r_sig, cnt(b, s, 4, dc + 1))
                nc.gpsimd.tensor_tensor(sg[:, dc % 2, :], sg[:, dc % 2, :], aa[:, dc % 2, :], ALU.mult
                                        ).then_inc(s_ready, 1)

            def lo(b, s, dc):
                pool.wait_ge(s_hi, cnt(b, s, 4, dc + 1))
                wait(pool, out_done, cnt(b, s - 1, 4, 4))
                nc.gpsimd.tensor_tensor(sTl[:, dc, :], sg[:, dc % 2, :], sTh[:, dc, :].bitcast(F32),
                                        ALU.subtract).then_inc(s_split, 1)

            def scatter(b, s, first, last):
                if first == 0:
                    v = 16 * (6 + (4 * b + s) // 2) if isinstance(b, int) else b * 32 + (6 + s // 2) * 16
                    gate(pool, (slot_ready, cnt(b, s, 2, 2)), (cleared[0], v), (cleared[1], v))
                for i in range(first, last):
                    j, g = i // (2 * G), i // 2 % G
                    nc.gpsimd.indirect_dma_start(
                        out=pages[g], out_offset=bass.IndirectOffsetOnAxis(ap=sidx[:, s % 2, i:i + 1], axis=0),
                        in_=h2[:, s % 2, j, :], in_offset=None).then_inc(scattered[s % 2], 16)

            def step(b, s, first):
                old = not (first and s < 2)
                rstd(f_var, vaf, h_ready, rsf, f_rstd, b, s + 1)
                receive(b, s, 0)
                lo(b, s, 0)
                rstd(g_var, vag, z_ready, rsg, g_rstd, b, s + 1)
                if not (first and s == 0):
                    rstd(b_var, vab, h2_ready, rsb, b_rstd, b, s - 1)
                if old:
                    scatter(b, s - 2, 0, 5)
                receive(b, s, 1)
                if old:
                    scatter(b, s - 2, 5, 7)
                lo(b, s, 1)
                if old:
                    scatter(b, s - 2, 7, 10)
                receive(b, s, 2)
                if old:
                    scatter(b, s - 2, 10, 12)
                lo(b, s, 2)
                if old:
                    scatter(b, s - 2, 12, 16)
                receive(b, s, 3)
                lo(b, s, 3)

            rstd(f_var, vaf, h_ready, rsf, f_rstd, 0, 0)
            rstd(g_var, vag, z_ready, rsg, g_rstd, 0, 0)
            for s in range(4):
                step(0, s, True)
            with pool.Fori(1, B) as b:
                for s in range(4):
                    step(b, s, False)
            rstd(b_var, vab, h2_ready, rsb, b_rstd, B, -1)
            scatter(B, -2, 0, 16)
            scatter(B, -1, 0, 16)
            for par in range(2):
                pool.wait_ge(scattered[par], 2 * B * 16 * 16)

        @block.vector
        def _(dve):
            V = nc.vector

            def norm_front(b, s, part):
                u = s % 4
                if part == 0:
                    dve.wait_ge(x_in[u], 16 * (b + s // 4 + 1) if isinstance(b, int) else b * 16 + (s // 4 + 1) * 16)
                    for j in range(TJ):
                        wait(dve, f_aggr, cnt(b, s - 1, 4, 4))
                        V.bn_stats(stf[:, j, :], xin[:, u, j, :]).then_inc(f_stats, 1)
                    for j in range(TJ):
                        gate(dve, (f_stats, cnt(b, s, 4, j + 1)),
                             (f_var, cnt(b, s - 1, 1, 1)), (h_half, cnt(b, s - 1, 4, 4)))
                        V.bn_aggr(mvf[:, j, :], stf[:, j, :]).then_inc(f_aggr, 1)
                    dve.wait_ge(f_aggr, cnt(b, s, 4, 4))
                    wait(dve, f_rstd, cnt(b, s - 1, 1, 1))
                    V.tensor_scalar(vaf[:], mvf[:, :, 1], EPS, None, ALU.add).then_inc(f_var, 1)
                elif part == 1:
                    if s % 4 == 0:
                        row = b + s // 4
                        dve.wait_ge(modf_in, 16 * (row + 1) if isinstance(b, int) else b * 16 + (s // 4 + 1) * 16)
                    wait(dve, frontT_done, cnt(b, s - 1, 4, 4))
                    wait(dve, logit_done, cnt(b, s - 3, 1, 1))
                    for j in range(TJ):
                        V.scalar_tensor_tensor(out=hb[:, j, :], in0=xin[:, u, j, :], scalar=mvf[:, j, 0:1],
                                               in1=mod[:, CA1, :], op0=ALU.subtract, op1=ALU.mult).then_inc(h_half, 1)
                elif part == 2:
                    dve.wait_ge(f_rstd, cnt(b, s, 1, 1))
                    for j in range(TJ):
                        dve.wait_ge(h_half, cnt(b, s, 4, j + 1))
                        V.scalar_tensor_tensor(out=hb[:, j, :], in0=hb[:, j, :], scalar=rsf[:, j:j + 1],
                                               in1=mod[:, SA, :], op0=ALU.mult, op1=ALU.add).then_inc(h_ready, 1)
                    for j in range(TJ):
                        dve.wait_ge(h_ready, cnt(b, s, 4, j + 1))
                        wait(dve, g_aggr, cnt(b, s - 1, 4, 4))
                        V.bn_stats(stg[:, j, :], hb[:, j, :]).then_inc(g_stats, 1)
                    for j in range(TJ):
                        gate(dve, (g_stats, cnt(b, s, 4, j + 1)),
                             (g_var, cnt(b, s - 1, 1, 1)), (g_nm, cnt(b, s - 1, 1, 1)))
                        V.bn_aggr(mvg[:, j, :], stg[:, j, :]).then_inc(g_aggr, 1)
                    dve.wait_ge(g_aggr, cnt(b, s, 4, 4))
                    wait(dve, g_rstd, cnt(b, s - 1, 1, 1))
                    V.tensor_scalar(vag[:], mvg[:, :, 1], EPS, None, ALU.add).then_inc(g_var, 1)
                else:
                    dve.wait_ge(g_rstd, cnt(b, s, 1, 1))
                    wait(dve, z_ready, cnt(b, s - 1, 4, 4))
                    V.scalar_tensor_tensor(out=nmg[:], in0=mvg[:, :, 0], scalar=-1.0, in1=rsg[:],
                                           op0=ALU.mult, op1=ALU.mult).then_inc(g_nm, 1)

            def split_x(b, s):
                for k in range(KC):
                    dve.wait_ge(x_hi, cnt(b, s + 1, 4, k + 1))
                    V.tensor_tensor(xTl[:, k, :], bank(s, FRONTT + k), xTh[:, k, :].bitcast(F32),
                                    ALU.subtract).then_inc(x_split, 1)

            def chunk(b, s, dc):
                u = dc % 2
                dve.wait_ge(k_biased, cnt(b, s, 4, dc + 1))
                dve.wait_ge(proj_done, cnt(b, s, 12, 3 * dc + 2))
                wait(dve, tfkv, cnt(b, s, 4, dc))
                wait(dve, wk_ready, cnt(b, s, 4, dc))
                V.scalar_tensor_tensor(out=kv[:], in0=bank(s, PROJ[dc] + 1), scalar=bias[:, 1, dc:dc + 1],
                                       in1=kb[:], op0=ALU.add, op1=ALU.mult).then_inc(kv_ready, 1)
                wait(dve, wkv_ready, cnt(b, s - 1, 4, dc + 1))
                wait(dve, scan, cnt(b, s - 1, 4, dc + 1))
                if s == 0:
                    V.memset(cs[:, dc, 0:1], 0.0).then_inc(carry, 1)
                else:
                    V.tensor_copy(cs[:, dc, 0:1], cs[:, dc, TT:TT + 1]).then_inc(carry, 1)
                dve.wait_ge(kv_ready, cnt(b, s, 4, dc + 1))
                wait(dve, scan, cnt(b, s, 4, dc))
                V.scalar_tensor_tensor(out=wk[:], in0=kv[:], scalar=gs[:, dc, s:s + 1],
                                       in1=pw[:, dc, :], op0=ALU.mult, op1=ALU.mult).then_inc(wk_ready, 1)
                dve.wait_ge(wk_ready, cnt(b, s, 4, dc + 1))
                dve.wait_ge(carry, cnt(b, s, 4, dc + 1))
                V.tensor_tensor_scan(cs[:, dc, 1:TT + 1], ones[:, 0:1].to_broadcast([P, TT]), wk[:],
                                     cs[:, dc, 0:1], ALU.mult, ALU.add).then_inc(scan, 1)
                dve.wait_ge(scan, cnt(b, s, 4, dc + 1))
                dve.wait_ge(tfkv, cnt(b, s, 4, dc + 1))
                V.scalar_tensor_tensor(out=aa[:, u, :], in0=cs[:, dc, 0:TT], scalar=tdc[:, dc:dc + 1],
                                       in1=aa[:, u, :], op0=ALU.mult, op1=ALU.add).then_inc(wkv_ready, 1)

            def wo(b, part):
                if part == 0:
                    dve.wait_ge(ga_in, (b + 1) * 16 if isinstance(b, int) else b * 16 + 16)
                    dve.wait_ge(wo_in, (b + 1) * 16 if isinstance(b, int) else b * 16 + 16)
                    V.tensor_tensor(wo_s, wo_s, mod[:, GA:GA + 1, :].to_broadcast([P, KC, C]),
                                    ALU.mult).then_inc(wo_scaled, 1)
                else:
                    dve.wait_ge(wo_hi, b + 1)
                    V.tensor_tensor(wol[:], wo_s, woh[:].bitcast(F32), ALU.subtract).then_inc(wo_split, 1)

            def residual(b, s):
                u = s % 4
                for j in range(TJ):
                    dve.wait_ge(out_done, cnt(b, s, 4, j + 1))
                    V.tensor_tensor(xin[:, u, j, :], bank(s + 1, OUTP + j), xin[:, u, j, :],
                                    ALU.add).then_inc(x1_ready, 1)
                    dve.wait_ge(x1_ready, cnt(b, s, 4, j + 1))
                    wait(dve, b_aggr, cnt(b, s - 1, 4, 4))
                    V.bn_stats(stb[:, j, :], xin[:, u, j, :]).then_inc(b_stats, 1)
                for j in range(TJ):
                    gate(dve, (b_stats, cnt(b, s, 4, j + 1)),
                         (b_var, cnt(b, s - 1, 1, 1)), (h2_half, cnt(b, s - 1, 4, 4)))
                    V.bn_aggr(mvb[:, j, :], stb[:, j, :]).then_inc(b_aggr, 1)
                dve.wait_ge(b_aggr, cnt(b, s, 4, 4))
                wait(dve, b_rstd, cnt(b, s - 1, 1, 1))
                V.tensor_scalar(vab[:], mvb[:, :, 1], EPS, None, ALU.add).then_inc(b_var, 1)

            def modulate(b, s):
                u = s % 2
                if s == 0:
                    dve.wait_ge(modb_in, (b + 1) * 16 if isinstance(b, int) else b * 16 + 16)
                if s in (-1, 1):
                    dve.wait_ge(wo_split, B if isinstance(b, int) and b == B else b + 1)
                wait(dve, scattered[u], dcnt(b, s - 2, 16))
                wait(dve, backT_done, cnt(b, s - 2, 4, 4))
                for j in range(TJ):
                    V.scalar_tensor_tensor(out=h2[:, u, j, :], in0=xin[:, s % 4, j, :], scalar=mvb[:, j, 0:1],
                                           in1=mod[:, CB1, :], op0=ALU.subtract, op1=ALU.mult).then_inc(h2_half, 1)
                dve.wait_ge(b_rstd, cnt(b, s, 1, 1))
                for j in range(TJ):
                    dve.wait_ge(h2_half, cnt(b, s, 4, j + 1))
                    V.scalar_tensor_tensor(out=h2[:, u, j, :], in0=h2[:, u, j, :], scalar=rsb[:, j:j + 1],
                                           in1=mod[:, SB, :], op0=ALU.mult, op1=ALU.add).then_inc(h2_ready, 1)

            def topk(b, s):
                for r in range(R):
                    if r == 0:
                        gate(dve, (lg_copied, cnt(b, s, 1, 1)),
                             (top_idx, cnt(b, s - 1, 8, 8)), (top_kept, cnt(b, s - 1, 1, 1)))
                    V.max(m8[:, r, :], lg[:, r]).then_inc(top_max, 1)
                for r in range(R):
                    gate(dve, (top_max, cnt(b, s, 8, r + 1)), (idx_f, cnt(b, s - 1, 1, 1)))
                    V.max_index(i8[:, r, :], m8[:, r, :], lg[:, r]).then_inc(top_idx, 1)
                wait(dve, lg_out, cnt(b, s - 1, 16, 16))
                V.tensor_copy(lgt[:, R * E:].rearrange("p (r k) -> p r k", k=2), m8[:, :, 0:2]
                              ).then_inc(top_kept, 1)
                dve.wait_ge(top_idx, cnt(b, s, 8, 8))
                wait(dve, hit, cnt(b, s - 1, 2, 2))
                V.tensor_copy(ixf[:], i8[:, :, 0:2]).then_inc(idx_f, 1)
                dve.wait_ge(idx_f, cnt(b, s, 1, 1))
                wait(dve, slot_ready, cnt(b, s - 1, 2, 2))
                for k, m in enumerate((hit1, hit2)):
                    V.tensor_tensor(m[:], iota[:].unsqueeze(1).to_broadcast([P, R, E]),
                                    ixf[:, :, k:k + 1].to_broadcast([P, R, E]), ALU.is_equal).then_inc(hit, 1)
                dve.wait_ge(hit, cnt(b, s, 2, 2))
                wait(dve, rank_done, cnt(b, s - 1, 1, 1))
                V.tensor_tensor(hits[:].rearrange("p j e -> p (j e)"), hit1[:].rearrange("p r e -> p (r e)"),
                                hit2[:].rearrange("p r e -> p (r e)"), ALU.add).then_inc(hits_ready, 1)

            def place(b, s):
                n = [0]

                def op(ins):
                    n[0] += 1
                    ins.then_inc(page_op, 1)
                    return n[0]

                def after(k):
                    dve.wait_ge(page_op, cnt(b, s, PGOPS, k))

                o = bank(s + 2, RANK)
                dve.wait_ge(rank_done, cnt(b, s, 1, 1))
                wait(dve, page_op, cnt(b, s, PGOPS, 0))
                wait(dve, hist_out, cnt(b, s - 1, 16, 16))
                V.tensor_tensor(tot[:], o[:, TJ * GE:(TJ + 1) * GE], used[:], ALU.add).then_inc(rank_read, 1)
                V.tensor_tensor(qq[:], o[:, 0:TJ * GE].rearrange("p (j e) -> p j e", j=TJ),
                                used[:].unsqueeze(1).to_broadcast([P, TJ, GE]), ALU.add).then_inc(rank_read, 1)
                dve.wait_ge(rank_read, cnt(b, s, 2, 1))
                k = op(V.tensor_scalar(two[:], tot[:], 2.0 * PAGE, None, ALU.is_gt))
                after(k)
                new = op(V.scalar_tensor_tensor(out=alloc[:, 1, :], in0=tot[:], scalar=1.0 * PAGE, in1=two[:],
                                                op0=ALU.is_gt, op1=ALU.add))
                after(new)
                for g in range(G):
                    k = op(V.tensor_tensor_scan(incl[:, g * E:(g + 1) * E], ones[:, 0:1].to_broadcast([P, E]),
                                                alloc[:, 1, g * E:(g + 1) * E], fre[:, g:g + 1], ALU.mult, ALU.add))
                after(k)
                k = op(V.tensor_tensor(alloc[:, 0, :], incl[:], alloc[:, 1, :], ALU.subtract))
                kf = op(V.tensor_copy(fre[:], incl[:, E - 1:GE:E]))
                after(k)
                k = op(V.scalar_tensor_tensor(out=dpg[:], in0=alloc[:, 0, :], scalar=-1.0, in1=cur[:],
                                              op0=ALU.add, op1=ALU.subtract))
                after(k)
                dve.wait_ge(rank_read, cnt(b, s, 2, 2))
                k = op(V.scalar_tensor_tensor(out=ee[:], in0=qq[:], scalar=1.0 * PAGE,
                                              in1=dpg[:].unsqueeze(1).to_broadcast([P, TJ, GE]),
                                              op0=ALU.is_ge, op1=ALU.mult))
                after(k)
                k = op(V.tensor_tensor(ee[:], ee[:], cur[:].unsqueeze(1).to_broadcast([P, TJ, GE]), ALU.add))
                ku = op(V.scalar_tensor_tensor(out=used[:], in0=alloc[:, 1, :], scalar=-1.0 * PAGE, in1=tot[:],
                                               op0=ALU.mult, op1=ALU.add))
                kd = op(V.scalar_tensor_tensor(out=dpg[:], in0=incl[:], scalar=-1.0, in1=cur[:],
                                               op0=ALU.add, op1=ALU.subtract))
                after(k)
                k = op(V.scalar_tensor_tensor(out=ee[:], in0=ee[:], scalar=1.0 * PAGE, in1=qq[:],
                                              op0=ALU.mult, op1=ALU.add))
                after(kd)
                kd = op(V.scalar_tensor_tensor(out=dpg[:], in0=alloc[:, 1, :], scalar=0.0, in1=dpg[:],
                                               op0=ALU.is_gt, op1=ALU.mult))
                after(kd)
                kc = op(V.tensor_tensor(cur[:], cur[:], dpg[:], ALU.add))
                ev = ee[:].rearrange("p j (g e) -> p (j g) e", g=G)
                after(k)
                for i, m in enumerate((hit1, hit2)):
                    k = op(V.tensor_tensor(m[:], m[:], ev, ALU.mult))
                    if i == 0:
                        k1 = k
                assert n[0] == PGOPS - 1
                after(k1 + 1)
                wait(dve, slot_ready, cnt(b, s, 2, 0))
                k = op(V.tensor_reduce(slf[:, 0, :], hit1[:], AX_X, ALU.add))
                V.tensor_reduce(slf[:, 1, :], hit2[:], AX_X, ALU.add).then_inc(slot_ready, 1)
                after(k)
                dve.wait_ge(slot_ready, cnt(b, s, 2, 1))
                wait(dve, scattered[s % 2], dcnt(b, s - 2, 16))
                wait(dve, slots_out[s % 2], dcnt(b, s - 2))
                V.tensor_copy(sidx[:, s % 2, :].rearrange("p (r k) -> p k r", k=2), slf[:]).then_inc(slot_ready, 1)

            def step(b, s, first):
                norm_front(b, s + 1, 0)
                if not (first and s < 2):
                    topk(b, s - 2)
                norm_front(b, s + 1, 1)
                chunk(b, s, 0)
                norm_front(b, s + 1, 2)
                if s == 0:
                    wo(b, 0)
                if not (first and s == 0):
                    residual(b, s - 1)
                norm_front(b, s + 1, 3)
                if not (first and s < 2):
                    place(b, s - 2)
                if s == 0:
                    wo(b, 1)
                chunk(b, s, 1)
                if not (first and s == 0):
                    modulate(b, s - 1)
                chunk(b, s, 2)
                chunk(b, s, 3)
                split_x(b, s)

            for part in range(4):
                norm_front(0, 0, part)
            split_x(0, -1)
            for s in range(4):
                step(0, s, True)
            with dve.Fori(1, B) as b:
                for s in range(4):
                    step(b, s, False)
            topk(B, -2)
            residual(B, -1)
            place(B, -2)
            modulate(B, -1)
            topk(B, -1)
            place(B, -1)


def setup(nc, L, A):
    B, KC, C, E, GE = L["B"], L["KC"], L["C"], L["E"], L["GE"]
    ps, ident = L["ps"], L["ident"]
    names = ("xin", "hb", "wTh", "wTl", "pw", "gs", "kb", "kv", "wk", "h2", "rws", "iota", "ones", "tri",
             "oneb", "bias", "tdc", "tfc", "gmc", "btc", "half", "used", "cur", "fre", "zrow", "aa", "sg")
    (xin, hb, wTh, wTl, pw, gs, kb, kv, wk, h2, rws, iota, ones, tri,
     oneb, bias, tdc, tfc, gmc, btc, half, used, cur, fre, zrow, aa, sg) = (A[n] for n in names)
    raw = [xin[:, i] for i in range(1, 4)]
    wm = [h2[:, 0], h2[:, 1], xin[:, 0]]
    cin = aa[:, 0, 0:KC * B].rearrange("p (k b) -> p k b", k=KC)
    csig = aa[:, 1, 0:KC * B].rearrange("p (k b) -> p k b", k=KC)
    csil = sg[:, 0, 0:KC * B].rearrange("p (k b) -> p k b", k=KC)
    tdn = sg[:, 0, KC * B:KC * B + KC]
    mrow = [hb[0:B, i, :] for i in range(KC)] + [kb[0:B, :], sg[0:B, 1, :]]
    ORDER = (SA, CA1, GA, SB, CB1, GBH)

    with ExitStack() as ctx:
        def sem(name):
            return nc.alloc_semaphore(name)

        small_in, rw_in = sem("s_small_in"), sem("s_rw_in")
        raw_in = [sem(f"s_raw_in{i}") for i in range(3)]
        wm_in = [sem(f"s_wm_in{i}") for i in range(3)]
        mod_out = sem("s_mod_out")
        filled, sel = sem("s_filled"), sem("s_sel")
        sig, biased, hi, lo, bias_kept = sem("s_sig"), sem("s_biased"), sem("s_hi_w"), sem("s_lo_w"), sem("s_bias_kept")
        silu, modded, row_done, chain = sem("s_silu"), sem("s_modded"), sem("s_row_done"), sem("s_chain")
        scaled = sem("s_scaled")
        block = ctx.enter_context(nc.Block())

        @block.sync
        def _(sp):
            for i, t in enumerate((tdc, tfc, gmc, btc)):
                sp.dma_start(t[:], L["vec"][i]).then_inc(small_in, 16)
            sp.dma_start(aa[:, 0, 0:KC * B], L["cT"]).then_inc(small_in, 16)
            for w in range(3):
                sp.dma_start(raw[w], L["wkvr"][w].rearrange("(k p) d -> p k d", p=P)).then_inc(raw_in[w], 16)
            for i in range(6):
                if i >= 3:
                    sp.wait_ge(modded, i - 2)
                sp.dma_start(wm[i % 3], L["wmod"][:, i * C:(i + 1) * C].rearrange("(k p) d -> p k d", p=P)
                             ).then_inc(wm_in[i % 3], 16)
            sp.dma_start(rws[:], L["rw"].rearrange("(k p) e -> p k e", p=P)).then_inc(rw_in, 16)
            for i, r in enumerate(ORDER):
                sp.wait_ge(row_done, i + 1)
                sp.dma_start(L["mod_d"][:, r * C:(r + 1) * C], mrow[i]).then_inc(mod_out, 16)
            sp.wait_ge(mod_out, 96)
            sp.wait_ge(rw_in, 16)

        @block.gpsimd
        def _(pool):
            g = nc.gpsimd
            g.memset(ident[:], 0.0).then_inc(filled, 1)
            g.memset(tri[:], 1.0).then_inc(filled, 1)
            g.memset(oneb[:], 1.0)
            g.memset(ones[:], 1.0)
            g.memset(half[:], -0.5)
            g.memset(zrow[:], 0.0)
            g.memset(used[:], 1.0 * PAGE)
            g.memset(cur[:], 0.0)
            g.memset(fre[:], 0.0)
            g.iota(iota[:], [[1, E]], base=0, channel_multiplier=0, allow_small_or_imprecise_dtypes=True)
            pool.wait_ge(filled, 2)
            g.affine_select(out=ident[:], in_=ident[:], compare_op=ALU.not_equal, fill=1.0, base=0,
                            pattern=[[-1, P]], channel_multiplier=1)
            g.affine_select(out=tri[:], in_=tri[:], compare_op=ALU.is_gt, fill=0.0, base=0,
                            pattern=[[1, P]], channel_multiplier=-1)

        @block.scalar
        def _(act):
            act.wait_ge(small_in, 80)
            nc.scalar.activation(tdc[:], tdc[:], ACT.Sigmoid).then_inc(sig, 1)
            nc.scalar.activation(tfc[:], tfc[:], ACT.Sigmoid).then_inc(sig, 1)
            nc.scalar.activation(csig, cin, ACT.Sigmoid).then_inc(sig, 1)
            for w in range(3):
                act.wait_ge(scaled, KC * (w + 1))
                nc.scalar.copy(wTh[:, w], raw[w]).then_inc(hi, 1)

        @block.tensor
        def _(pe):
            for w in range(3):
                pe.wait_ge(raw_in[w], 16)
                if w == 0:
                    pe.wait_ge(small_in, 80)
                for dc in range(KC):
                    for k in range(KC):
                        at = w * KC + dc
                        last = nc.tensor.matmul(ps[:, 6, at:at + 1], raw[w][:, k, dc * P:(dc + 1) * P],
                                                btc[:, k:k + 1], start=(k == 0), stop=(k == KC - 1))
                last.then_inc(biased, 1)
            pe.wait_ge(silu, 1)
            for i in range(6):
                pe.wait_ge(wm_in[i % 3], 16 * (i // 3 + 1))
                for k in range(KC):
                    last = nc.tensor.matmul(ps[0:B, i, :], csil[:, k, :], wm[i % 3][:, k, :],
                                            start=(k == 0), stop=(k == KC - 1))
                last.then_inc(modded, 1)

        @block.vector
        def _(dve):
            V = nc.vector
            n = [0]

            def link(ins):
                n[0] += 1
                ins.then_inc(chain, 1)
                dve.wait_ge(chain, n[0])

            dve.wait_ge(sig, 3)
            V.tensor_tensor(csil, cin, csig, ALU.mult).then_inc(silu, 1)
            for w in range(3):
                dve.wait_ge(raw_in[w], 16)
                dve.wait_ge(biased, w + 1)
                for k in range(KC):
                    V.tensor_scalar(raw[w][:, k, :], raw[w][:, k, :], gmc[:, k:k + 1], None,
                                    ALU.mult).then_inc(scaled, 1)
            V.tensor_copy(bias[:].rearrange("p w k -> p (w k)"), ps[:, 6, 0:3 * KC])
            for w in range(3):
                dve.wait_ge(hi, w + 1)
                V.tensor_tensor(wTl[:, w], raw[w], wTh[:, w].bitcast(F32), ALU.subtract)
            V.memset(pw[:, :, 0:1], 1.0)
            V.memset(gs[:, :, 0:1], 1.0)
            link(V.tensor_copy(tdn, tdc[:]))
            m = 1
            while m < TT:
                V.tensor_tensor(pw[:, :, m:2 * m], pw[:, :, 0:m], tdn.unsqueeze(2).to_broadcast([P, KC, m]),
                                ALU.mult).then_inc(chain, 1)
                n[0] += 1
                dve.wait_ge(chain, n[0])
                link(V.tensor_tensor(tdn, tdn, tdn, ALU.mult))
                m *= 2
            for i in range(3):
                link(V.tensor_tensor(gs[:, :, i + 1:i + 2], gs[:, :, i:i + 1], tdn.unsqueeze(2), ALU.mult))
            for i, r in enumerate(ORDER):
                dve.wait_ge(modded, i + 1)
                p = ps[0:B, i, :]
                if r in (SA, SB):
                    V.tensor_copy(mrow[i], p).then_inc(row_done, 1)
                elif r in (CA1, CB1):
                    V.tensor_scalar(mrow[i], p, 1.0, None, ALU.add).then_inc(row_done, 1)
                else:
                    sign, size = kv[0:B, :], wk[0:B, :]
                    link(V.tensor_scalar(size, p, -1.0, None, ALU.mult))
                    link(V.tensor_tensor(size, size, p, ALU.max))
                    link(V.tensor_scalar(size, size, 0.25, 0.5 if r == GBH else 1.0, ALU.max, ALU.mult))
                    link(V.tensor_scalar(sign, p, 0.0, 2.0, ALU.is_ge, ALU.mult))
                    V.scalar_tensor_tensor(out=mrow[i], in0=sign, scalar=-1.0, in1=size, op0=ALU.add,
                                           op1=ALU.mult).then_inc(row_done, 1)
                    dve.wait_ge(row_done, i + 1)


def stage_b(nc, L):
    G, E, GE, STEPS, NPG = L["G"], L["E"], L["GE"], L["STEPS"], L["NPG"]
    wts = L["wts"]
    RR = STEPS * TJ * G
    with ExitStack() as ctx:
        def sb(name, shape, dt=F32):
            return ctx.enter_context(nc.sbuf_tensor(name, shape, dt))

        def sem(name):
            return ctx.enter_context(nc.semaphore(name))

        lga = sb("b_logits", [P, STEPS, TJ * GE + 16])
        lgt = sb("b_exp", [P, RR, E])
        top2 = sb("b_top2", [P, RR])
        hist = sb("b_hist", [P, STEPS, 2, GE])
        end = sb("b_end", [P, STEPS, GE])
        inside = sb("b_inside", [P, G, STEPS, E])
        bound = sb("b_bound", [P, G, STEPS, E])
        io = sb("b_iota", [P, E])
        pid = sb("b_page", [P, 2])
        own = sb("b_own", [P, G * 2])
        ownu = sb("b_ownu", [P, G * 2], U32)
        den = sb("b_den", [P, RR])
        rec = sb("b_rec", [P, RR])
        lg_in, hist_in, own_out = sem("b_lg_in"), sem("b_hist_in"), sem("b_own_out")
        numbered, shifted, exped, chain, owned = sem("b_numbered"), sem("b_shifted"), sem("b_exped"), sem("b_chain"), sem("b_owned")
        lv = lga[:, :, 0:TJ * GE].rearrange("p s (r e) -> p s r e", e=E)
        tv = lga[:, :, TJ * GE:].rearrange("p s (r k) -> p s r k", k=2)
        sv = lambda t: t.rearrange("p (s r) -> p s r", s=STEPS)
        wv = wts[:].rearrange("p (r k) -> p r k", k=2)
        block = ctx.enter_context(nc.Block())

        @block.sync
        def _(sp):
            sp.dma_start(hist[:].rearrange("p s a e -> p (s a e)"),
                         L["hist_d"].rearrange("s e -> (s e)").unsqueeze(0).to_broadcast([P, STEPS * 2 * GE])
                         ).then_inc(hist_in, 16)
            sp.dma_start(lga[:].rearrange("p s n -> p (s n)"), L["lg_d"]).then_inc(lg_in, 16)
            sp.wait_ge(owned, 1)
            sp.dma_start(L["own_d"].rearrange("i p -> p i"), ownu[:], allow_slow_non_contiguous=True).then_inc(own_out, 16)
            sp.wait_ge(own_out, 16)

        @block.gpsimd
        def _(pool):
            nc.gpsimd.iota(io[:], [[1, E]], base=0, channel_multiplier=0, allow_small_or_imprecise_dtypes=True)
            nc.gpsimd.iota(pid[:], [[P, 2]], base=0, channel_multiplier=1,
                           allow_small_or_imprecise_dtypes=True).then_inc(numbered, 1)

        @block.scalar
        def _(act):
            act.wait_ge(shifted, 1)
            nc.scalar.activation(lgt[:], lgt[:], ACT.Exp).then_inc(exped, 1)
            act.wait_ge(shifted, 2)
            nc.scalar.activation(top2[:], top2[:], ACT.Exp).then_inc(exped, 1)

        @block.vector
        def _(dve):
            V = nc.vector
            n = [0]

            def link(ins):
                n[0] += 1
                ins.then_inc(chain, 1)
                dve.wait_ge(chain, n[0])

            dve.wait_ge(lg_in, 16)
            V.tensor_tensor(lgt[:].rearrange("p (s r) e -> p s r e", s=STEPS), lv,
                            tv[:, :, :, 0:1].to_broadcast([P, STEPS, TJ * G, E]), ALU.subtract).then_inc(shifted, 1)
            V.tensor_tensor(sv(top2[:]), tv[:, :, :, 1], tv[:, :, :, 0], ALU.subtract).then_inc(shifted, 1)
            dve.wait_ge(hist_in, 16)
            dve.wait_ge(numbered, 1)
            link(V.tensor_tensor(end[:], hist[:, :, 0, :], hist[:, :, 1, :], ALU.add))
            for g in range(G):
                for c in range(2):
                    e = slice(g * E, (g + 1) * E)
                    link(V.tensor_scalar(bound[:, g], hist[:, :, 0, e], pid[:, c:c + 1], None, ALU.is_le))
                    link(V.scalar_tensor_tensor(out=inside[:, g], in0=end[:, :, e], scalar=pid[:, c:c + 1],
                                                in1=bound[:, g], op0=ALU.is_gt, op1=ALU.mult))
                    link(V.tensor_tensor(inside[:, g], inside[:, g],
                                         io[:].unsqueeze(1).to_broadcast([P, STEPS, E]), ALU.mult))
                    link(V.tensor_reduce(own[:, g * 2 + c:g * 2 + c + 1],
                                         inside[:, g].rearrange("p s e -> p (s e)"), AX_X, ALU.add))
            V.tensor_copy(ownu[:], own[:]).then_inc(owned, 1)
            dve.wait_ge(exped, 1)
            link(V.tensor_reduce(den[:], lgt[:], AX_X, ALU.add))
            link(V.reciprocal(rec[:], den[:]))
            V.tensor_copy(wv[:, :, 0], rec[:])
            dve.wait_ge(exped, 2)
            V.tensor_tensor(wv[:, :, 1], rec[:], top2[:], ALU.mult)


def stage_c(nc, g, L):
    KC, C, H, NPG, NPAGES, WROW = L["KC"], L["C"], L["H"], L["NPG"], L["NPAGES"], L["WROW"]
    ps, ident, pages, own_d, wex = L["ps"], L["ident"], L["pages"][g], L["own_d"], L["wex"][g]
    J, HC = PAGE // P, H // P
    GU = KC * 2 * H
    with ExitStack() as ctx:
        def sb(name, shape, dt=F32):
            return ctx.enter_context(nc.sbuf_tensor(f"c{g}_{name}", shape, dt))

        def sem(name):
            return ctx.enter_context(nc.semaphore(f"c{g}_{name}"))

        own = sb("own", [1, 2 * P], U32)
        wraw = sb("wraw", [P, 2, WROW])
        wh = sb("wh", [P, 2, WROW], F32R)
        wl = sb("wl", [P, 2, WROW], F32R)
        xp = sb("xp", [P, 2, J, C])
        xh = sb("xh", [P, 2, J, KC, P], F32R)
        xl = sb("xl", [P, 2, J, KC, P], F32R)
        sil = sb("sil", [P, J, H])
        hh = sb("hh", [P, J, H])
        hTh = sb("hTh", [P, J, HC, P], F32R)
        hTl = sb("hTl", [P, J, HC, P], F32R)
        y = sb("y", [P, 2, J, C])
        own_in = sem("own_in")
        w_in, x_in, y_out = ([sem(f"{n}{i}") for i in range(2)] for n in ("w_in", "x_in", "y_out"))
        gu_done, hT_done, xT_done, y_done = sem("gu_done"), sem("hT_done"), sem("xT_done"), sem("y_done")
        w_hi, w_lo = sem("w_hi"), sem("w_lo")
        x_hi, x_lo, silu, h_ready, h_hi, h_lo = (sem(n) for n in ("x_hi", "x_lo", "silu", "h_ready", "h_hi", "h_lo"))
        y_copied0, y_copied1 = sem("y_copied0"), sem("y_copied1")
        PARTS = ((0, GU // 2), (GU // 2, GU), (GU, WROW))
        prow = pages.rearrange("(q j) c -> q (j c)", j=J)

        def cp(it, s, per, k):
            return it * (2 * per) + (s * per + k)

        def cd(it, s):
            return it * 16 + (s // 2 + 1) * 16

        block = ctx.enter_context(nc.Block())

        @block.sync
        def _(sp):
            def load(it, s):
                u = s % 2
                gate(sp, (w_lo, cp(it, s - 2, 3, 3)))
                page = it * 2 + s
                e = sp.value_load(own[0:1, bass.ds(page, 1)], min_val=0, max_val=L["E"] - 1)
                sp.dma_start(wraw[:, u, :], wex[bass.ds(e * P, P), :]).then_inc(w_in[u], 16)
                wait(sp, xT_done, cp(it, s - 2, J, J))
                sp.dma_start(xp[:, u].rearrange("p j c -> p (j c)"), prow[bass.ds(page * P, P), :]
                             ).then_inc(x_in[u], 16)

            def store(it, s):
                wait(sp, y_copied0, cp(it, s, 1, 1))
                wait(sp, y_copied1, cp(it, s, 1, 1))
                page = it * 2 + s
                sp.dma_start(prow[bass.ds(page * P, P), :], y[:, s % 2].rearrange("p j c -> p (j c)")
                             ).then_inc(y_out[s % 2], 16)

            sp.dma_start(own[:], own_d[2 * g:2 * g + 2, :].rearrange("i p -> (i p)").unsqueeze(0)).then_inc(own_in, 16)
            sp.wait_ge(own_in, 16)
            load(0, 0)
            load(0, 1)

            def page(it, s, first):
                load(it, s + 2)
                if not (first and s == 0):
                    store(it, s - 1)

            for s in range(2):
                page(0, s, True)
            with sp.Fori(1, NPG // 2 - 1) as it:
                for s in range(2):
                    page(it, s, False)
            last = NPG // 2 - 1
            store(last, -1)
            store(last, 0)
            store(last, 1)
            for u in range(2):
                sp.wait_ge(y_out[u], 16 * (NPG // 2))

        @block.tensor
        def _(pe):
            def split3(o, lh, ll, rh, rl, first, last):
                nc.tensor.matmul(o, lh, rh, start=first, stop=False)
                nc.tensor.matmul(o, lh, rl, start=False, stop=False)
                return nc.tensor.matmul(o, ll, rh, start=False, stop=last)

            def turn_x(it, s, j):
                if j == 0:
                    pe.wait_ge(x_in[s % 2], cd(it, s))
                wait(pe, x_lo, cp(it, s - 1, J, j + 1))
                for k in range(KC):
                    last = nc.tensor.transpose(ps[:, 4 + j, k * P:(k + 1) * P],
                                               xp[:, s % 2, j, k * P:(k + 1) * P], ident[:])
                last.then_inc(xT_done, 1)

            def gate_up(it, s, j):
                u = s % 2
                pe.wait_ge(x_lo, cp(it, s, J, j + 1))
                if j == 0:
                    pe.wait_ge(w_lo, cp(it, s, 3, 2))
                wait(pe, h_ready, cp(it, s - 1, J, j + 1))
                for k in range(KC):
                    c = slice(k * 2 * H, (k + 1) * 2 * H)
                    last = split3(ps[:, j, :], xh[:, u, j, k, :], xl[:, u, j, k, :], wh[:, u, c], wl[:, u, c],
                                  k == 0, k == KC - 1)
                last.then_inc(gu_done, 1)

            def turn_h(it, s, j):
                pe.wait_ge(h_ready, cp(it, s, J, j + 1))
                wait(pe, h_lo, cp(it, s - 1, J, j + 1))
                for q in range(HC):
                    last = nc.tensor.transpose(ps[:, 2 + j, q * P:(q + 1) * P], hh[:, j, q * P:(q + 1) * P], ident[:])
                last.then_inc(hT_done, 1)

            def down(it, s, j):
                u = s % 2
                pe.wait_ge(h_lo, cp(it, s, J, j + 1))
                if j == 0:
                    pe.wait_ge(w_lo, cp(it, s, 3, 3))
                wait(pe, (y_copied0, y_copied1)[j], cp(it, s - 1, 1, 1))
                for q in range(HC):
                    c = slice(GU + q * C, GU + (q + 1) * C)
                    last = split3(ps[:, 6 + j, :], hTh[:, j, q, :], hTl[:, j, q, :], wh[:, u, c], wl[:, u, c],
                                  q == 0, q == HC - 1)
                last.then_inc(y_done, 1)

            def page(it, s, first, final=False):
                gate_up(it, s, 0)
                if not (first and s == 0):
                    down(it, s - 1, 1)
                turn_h(it, s, 0)
                if not final:
                    turn_x(it, s + 1, 0)
                    turn_x(it, s + 1, 1)
                gate_up(it, s, 1)
                down(it, s, 0)
                turn_h(it, s, 1)

            turn_x(0, 0, 0)
            turn_x(0, 0, 1)
            for s in range(2):
                page(0, s, True)
            with pe.Fori(1, NPG // 2 - 1) as it:
                for s in range(2):
                    page(it, s, False)
            last = NPG // 2 - 1
            page(last, 0, False)
            page(last, 1, False, True)
            down(last, 1, 1)

        @block.scalar
        def _(act):
            def whi(it, s, part):
                u, (a, z) = s % 2, PARTS[part]
                act.wait_ge(w_in[u], cd(it, s))
                if part == 2:
                    wait(act, y_done, cp(it, s - 2, J, J))
                else:
                    wait(act, gu_done, cp(it, s - 2, J, J))
                nc.scalar.copy(wh[:, u, a:z], wraw[:, u, a:z]).then_inc(w_hi, 1)

            def xhi(it, s, j):
                act.wait_ge(xT_done, cp(it, s, J, j + 1))
                wait(act, gu_done, cp(it, s - 2, J, j + 1))
                nc.scalar.copy(xh[:, s % 2, j].rearrange("p k t -> p (k t)"), ps[:, 4 + j, :]).then_inc(x_hi, 1)

            def swish(it, s, j):
                act.wait_ge(gu_done, cp(it, s, J, j + 1))
                wait(act, h_ready, cp(it, s - 1, J, j + 1))
                nc.scalar.activation(sil[:, j, :], ps[:, j, 0:H], ACT.Silu).then_inc(silu, 1)

            def hhi(it, s, j):
                act.wait_ge(hT_done, cp(it, s, J, j + 1))
                wait(act, y_done, cp(it, s - 1, J, j + 1))
                nc.scalar.copy(hTh[:, j].rearrange("p q t -> p (q t)"), ps[:, 2 + j, 0:H]).then_inc(h_hi, 1)

            def ycopy(it, s):
                act.wait_ge(y_done, cp(it, s, J, 1))
                wait(act, y_out[s % 2], cd(it, s - 2))
                nc.scalar.copy(y[:, s % 2, 0, :], ps[:, 6, :]).then_inc(y_copied0, 1)

            def page(it, s, final=False):
                if not final:
                    whi(it, s + 1, 0)
                swish(it, s, 0)
                if not final:
                    whi(it, s + 1, 1)
                hhi(it, s, 0)
                if not final:
                    xhi(it, s + 1, 0)
                    xhi(it, s + 1, 1)
                    whi(it, s + 1, 2)
                swish(it, s, 1)
                hhi(it, s, 1)
                ycopy(it, s)

            for part in range(3):
                whi(0, 0, part)
            xhi(0, 0, 0)
            xhi(0, 0, 1)
            for s in range(2):
                page(0, s)
            with act.Fori(1, NPG // 2 - 1) as it:
                for s in range(2):
                    page(it, s)
            last = NPG // 2 - 1
            page(last, 0)
            page(last, 1, True)

        @block.vector
        def _(dve):
            V = nc.vector

            def wlo(it, s, part):
                u, (a, z) = s % 2, PARTS[part]
                dve.wait_ge(w_hi, cp(it, s, 3, part + 1))
                V.tensor_tensor(wl[:, u, a:z], wraw[:, u, a:z], wh[:, u, a:z].bitcast(F32),
                                ALU.subtract).then_inc(w_lo, 1)

            def xlo(it, s, j):
                dve.wait_ge(x_hi, cp(it, s, J, j + 1))
                V.tensor_tensor(xl[:, s % 2, j].rearrange("p k t -> p (k t)"), ps[:, 4 + j, :],
                                xh[:, s % 2, j].rearrange("p k t -> p (k t)").bitcast(F32),
                                ALU.subtract).then_inc(x_lo, 1)

            def hidden(it, s, j):
                dve.wait_ge(silu, cp(it, s, J, j + 1))
                wait(dve, hT_done, cp(it, s - 1, J, j + 1))
                V.tensor_tensor(hh[:, j, :], ps[:, j, H:2 * H], sil[:, j, :], ALU.mult).then_inc(h_ready, 1)

            def hlo(it, s, j):
                dve.wait_ge(h_hi, cp(it, s, J, j + 1))
                V.tensor_tensor(hTl[:, j].rearrange("p q t -> p (q t)"), ps[:, 2 + j, 0:H],
                                hTh[:, j].rearrange("p q t -> p (q t)").bitcast(F32),
                                ALU.subtract).then_inc(h_lo, 1)

            def ycopy(it, s):
                dve.wait_ge(y_done, cp(it, s, J, 2))
                wait(dve, y_out[s % 2], cd(it, s - 2))
                V.tensor_copy(y[:, s % 2, 1, :], ps[:, 7, :]).then_inc(y_copied1, 1)

            def page(it, s, first, final=False):
                if not final:
                    wlo(it, s + 1, 0)
                hidden(it, s, 0)
                if not (first and s == 0):
                    ycopy(it, s - 1)
                hlo(it, s, 0)
                if not final:
                    wlo(it, s + 1, 1)
                    xlo(it, s + 1, 0)
                    xlo(it, s + 1, 1)
                    wlo(it, s + 1, 2)
                hidden(it, s, 1)
                hlo(it, s, 1)

            for part in range(3):
                wlo(0, 0, part)
            xlo(0, 0, 0)
            xlo(0, 0, 1)
            for s in range(2):
                page(0, s, True)
            with dve.Fori(1, NPG // 2 - 1) as it:
                for s in range(2):
                    page(it, s, False)
            last = NPG // 2 - 1
            page(last, 0, False)
            page(last, 1, False, True)
            ycopy(last, 1)


def stage_d(nc, L):
    B, C, G, N = L["B"], L["C"], L["G"], L["N"]
    pages, x1_d, outf, mod_d, slots_d, wts = L["pages"], L["x1_d"], L["outf"], L["mod_d"], L["slots_d"], L["wts"]
    TPB = 4 * TJ
    K = 2 * G
    with ExitStack() as ctx:
        def sb(name, shape, dt=F32):
            return ctx.enter_context(nc.sbuf_tensor(f"d_{name}", shape, dt))

        def sem(name):
            return ctx.enter_context(nc.semaphore(f"d_{name}"))

        NB = 4
        yk = sb("yk", [P, NB, K, C])
        xr = sb("xr", [P, NB, C])
        acc = sb("acc", [P, NB, C])
        res = sb("res", [P, NB, C])
        gb = sb("gb", [P, C])
        si = sb("si", [P, TPB * K], U32)
        wi = sb("wi", [P, TPB * K])
        gb_in, si_in = sem("gb_in"), sem("si_in")
        y_in, x_in, out_done = ([sem(f"{n}{i}") for i in range(NB)] for n in ("y_in", "x_in", "out_done"))
        wi_ready, t0, t1, t2, t3, gated, summed = (
            sem(n) for n in ("wi_ready", "t0", "t1", "t2", "t3", "gated", "summed"))

        def ct(b, t, k=1):
            return b * TPB + (t + k)

        def cb(b, t, per=1):
            return b * (TPB // NB * 16 * per) + (t // NB + 1) * (16 * per)

        block = ctx.enter_context(nc.Block())

        @block.sync
        def _(sp):
            def tile(b, t):
                wait(sp, summed, ct(b, t - NB))
                row = b * (TPB * P) + t * P
                sp.dma_start(xr[:, t % NB], x1_d[bass.ds(row, P), :]).then_inc(x_in[t % NB], 16)

            def store(b, t):
                wait(sp, summed, ct(b, t))
                row = b * (TPB * P) + t * P
                sp.dma_start(outf[bass.ds(row, P), :], res[:, t % NB]).then_inc(out_done[t % NB], 16)

            def row(b, first):
                if not first:
                    gate(sp, (gated, ct(b, -1)), *((y_in[i], cb(b, i - NB, K)) for i in range(NB)))
                sp.dma_start(si[:], slots_d[:, bass.ds(b * (TPB * K), TPB * K)]).then_inc(si_in, 16)
                sp.dma_start(gb[:], mod_d[bass.ds(b, 1), GBH * C:(GBH + 1) * C].to_broadcast([P, C])).then_inc(gb_in, 16)
                for t in range(TPB):
                    tile(b, t)
                    if not (first and t < 2):
                        store(b, t - 2)

            row(0, True)
            with sp.Fori(1, B) as b:
                row(b, False)
            store(B, -2)
            store(B, -1)
            for i in range(NB):
                sp.wait_ge(out_done[i], 16 * TPB // NB * B)

        @block.gpsimd
        def _(pool):
            def row(b, first):
                gate(pool, (si_in, (b + 1) * 16 if isinstance(b, int) else b * 16 + 16))
                for t in range(TPB):
                    if not (first and t < NB):
                        gate(pool, (gated, ct(b, t - NB)))
                    for k in range(K):
                        nc.gpsimd.indirect_dma_start(
                            out=yk[:, t % NB, k, :], out_offset=None, in_=pages[k // 2],
                            in_offset=bass.IndirectOffsetOnAxis(ap=si[:, t * K + k:t * K + k + 1], axis=0)
                        ).then_inc(y_in[t % NB], 16)

            row(0, True)
            with pool.Fori(1, B) as b:
                row(b, False)

        @block.vector
        def _(dve):
            V = nc.vector

            def row(b, first):
                n = TPB * K
                wait(dve, gated, ct(b, -1))
                V.tensor_copy(wi[:], wts[:, bass.ds(b * n, n)]).then_inc(wi_ready, 1)
                dve.wait_ge(wi_ready, b + 1)
                dve.wait_ge(gb_in, (b + 1) * 16 if isinstance(b, int) else b * 16 + 16)
                for t in range(TPB):
                    u = t % NB
                    dve.wait_ge(y_in[u], cb(b, t, K))
                    wait(dve, summed, ct(b, t - NB))
                    V.tensor_scalar(acc[:, u], yk[:, u, 0], wi[:, t * K:t * K + 1], None, ALU.mult).then_inc(t0, 1)
                    for k, (before, after) in enumerate(((t0, t1), (t1, t2), (t2, t3)), 1):
                        dve.wait_ge(before, ct(b, t))
                        V.scalar_tensor_tensor(out=acc[:, u], in0=yk[:, u, k], scalar=wi[:, t * K + k:t * K + k + 1],
                                               in1=acc[:, u], op0=ALU.mult, op1=ALU.add).then_inc(after, 1)
                    dve.wait_ge(t3, ct(b, t))
                    V.tensor_tensor(acc[:, u], acc[:, u], gb[:], ALU.mult).then_inc(gated, 1)
                    dve.wait_ge(gated, ct(b, t))
                    dve.wait_ge(x_in[u], cb(b, t))
                    wait(dve, out_done[u], cb(b, t - NB))
                    V.tensor_tensor(res[:, u], acc[:, u], xr[:, u], ALU.add).then_inc(summed, 1)

            row(0, True)
            with dve.Fori(1, B) as b:
                row(b, False)


def kernel(**inputs):
    import numpy as np
    from concourse import bacc
    from concourse.bass_utils import run_bass_kernel_spmd

    a = {k: np.asarray(v) for k, v in inputs.items()}
    x = a["L0_attn_x"]
    E, C, H = a["L0_ffn_wg0"].shape
    KC, HC = C // P, H // P

    def experts(i):
        wg, wu = (a[f"L0_ffn_{n}{i}"].reshape(E, KC, P, H) for n in ("wg", "wu"))
        gu = np.stack([wg, wu], axis=3).transpose(0, 2, 1, 3, 4).reshape(E * P, KC * 2 * H)
        wd = a[f"L0_ffn_wd{i}"].reshape(E, HC, P, C).transpose(0, 2, 1, 3).reshape(E * P, HC * C)
        return np.concatenate([gu, wd], axis=1)

    arrays = {
        "x": x,
        "vec": np.stack([a[f"L0_attn_{n}"].reshape(KC, P).T
                         for n in ("time_decay", "time_first", "ln_gamma", "ln_beta")]),
        "wkvr": np.stack([a[f"L0_attn_W{n}"].T for n in "kvr"]),
        "wo": a["L0_attn_Wo"].T,
        "rw": np.concatenate([a["L0_ffn_router_w0"], a["L0_ffn_router_w1"]], axis=1),
        "wex0": experts(0),
        "wex1": experts(1),
        "cT": a["L0_c"].T.reshape(KC, P, -1).transpose(1, 0, 2).reshape(P, -1),
        "wmod": a["L0_wmod"],
    }
    arrays = {n: np.ascontiguousarray(v) for n, v in arrays.items()}
    nc = bacc.Bacc("TRN2", target_bir_lowering=False, num_devices=1)
    t = {n: nc.dram_tensor(n, v.shape, mybir.dt.from_np(v.dtype), kind="ExternalInput").ap()
         for n, v in arrays.items()}
    out = nc.dram_tensor("out", x.shape, mybir.dt.from_np(x.dtype), kind="ExternalOutput").ap()
    build(nc, t["x"], t["vec"], t["wkvr"], t["wo"], t["rw"],
          [t["wex0"], t["wex1"]], t["cT"], t["wmod"], out)
    r = run_bass_kernel_spmd(nc, [arrays], core_ids=[0])
    return r.results[0]["out"]
```

```python
from contextlib import ExitStack

import concourse.bass as bass
import concourse.mybir as mybir

P = 128
F32 = mybir.dt.float32
F32R = mybir.dt.float32r
BF16 = mybir.dt.bfloat16
U32 = mybir.dt.uint32
ALU = mybir.AluOpType
ACT = mybir.ActivationFunctionType
AX_X = mybir.AxisListType.X

EPS = 1e-5
TT = 512
TJ = TT // P
PAGE = 256
BANK = 512
NBANK = 8

CA1, SA, CB1, SB, GA, GBH = range(6)

PROJ = ((0, 1, 2), (8, 9, 10), (11, 12, 13), (18, 20, 21))
OUTP, RANK, BACKT, LOGIT, FRONTT = 3, 7, 14, 19, 22
GROUPS = 26


def wait(eng, sem, value):
    if isinstance(value, int) and value <= 0:
        return
    eng.wait_ge(sem, value)


def gate(eng, *waits):
    waits = [(sem, value if isinstance(value, int) else eng.to_reg(value)) for sem, value in waits]
    if not isinstance(waits[0][1], int):
        eng.wait_ge(waits[0][0], 1)
    for sem, value in waits:
        wait(eng, sem, value)


def cnt(b, s, per, k):
    if isinstance(b, int):
        return (4 * b + s) * per + k
    return b * (4 * per) + (s * per + k)


def dcnt(b, s, k=1):
    q = 16 * k
    if isinstance(b, int):
        return (2 * b + s // 2 + 1) * q
    return b * (2 * q) + (s // 2 + 1) * q


def build(nc, x, vec, wkvr, wo, rw, wex, cT, wmod, out):
    B, T, C = x.shape
    N = B * T
    KC = C // P
    STEPS = N // TT
    SPB = T // TT
    G, E = 2, rw.shape[1] // 2
    GE = G * E
    H = 256
    WROW = KC * 2 * H + (H // P) * C
    NPG = 2 * N // PAGE + E
    NPG += NPG % 2
    FILL = 8
    NPAGES = FILL * (4 + 2 * B)
    assert SPB == 4 and KC == 4 and C == BANK and NPG <= 2 * P and NPG <= NPAGES and E & (E - 1) == 0
    assert GROUPS * SPB % NBANK == 0

    xf = x.rearrange("b t c -> (b t) c")
    outf = out.rearrange("b t c -> (b t) c")
    x1_d = nc.dram_tensor("x1_d", (N, C), F32, kind="Internal").ap()
    lg_d = nc.dram_tensor("lg_d", (P, STEPS * (4 * GE + 16)), F32, kind="Internal").ap()
    slots_d = nc.dram_tensor("slots_d", (P, STEPS * 16), U32, kind="Internal").ap()
    hist_d = nc.dram_tensor("hist_d", (STEPS, GE), F32, kind="Internal").ap()
    mod_d = nc.dram_tensor("mod_d", (B, 6 * C), F32, kind="Internal").ap()
    key_d = nc.dram_tensor("key_d", (2, G * 2, P), F32, kind="Internal").ap()
    order_d = nc.dram_tensor("order_d", (G, 2, 2, P), U32, kind="Internal").ap()
    pages = [nc.dram_tensor(f"pages{g}_d", (NPAGES * PAGE, C), F32, kind="Internal").ap()
             for g in range(G)]

    with ExitStack() as whole:
        ident = whole.enter_context(nc.sbuf_tensor("ident", [P, P], F32))
        ps = whole.enter_context(nc.psum_tensor("ps", [P, NBANK, BANK], F32))
        h2 = whole.enter_context(nc.sbuf_tensor("h2", [P, 2, TJ, C], F32))
        sidx = whole.enter_context(nc.sbuf_tensor("sidx", [P, 2, TJ * G * 2], U32))

        with nc.cleanup_on_exit():
            stage_a(nc, locals())
        wts = whole.enter_context(nc.sbuf_tensor("wts", [P, STEPS * 16], F32))
        stage_b(nc, locals())
        for g in range(G):
            stage_c(nc, g, locals())
        stage_d(nc, locals())


def stage_a(nc, L):
    B, KC, GE, E, G, C = L["B"], L["KC"], L["GE"], L["E"], L["G"], L["C"]
    N, FILL = L["N"], L["FILL"]
    ps, ident = L["ps"], L["ident"]
    slots_d = L["slots_d"]
    xf, x1_d, lg_d, hist_d, mod_d, pages = L["xf"], L["x1_d"], L["lg_d"], L["hist_d"], L["mod_d"], L["pages"]
    R = TJ * G

    with ExitStack() as ctx:
        def sb(name, shape, dt=F32):
            return ctx.enter_context(nc.sbuf_tensor(name, shape, dt))

        def sem(name):
            return nc.alloc_semaphore(name)

        xin = sb("xin", [P, 4, TJ, C])
        hb = sb("hb", [P, TJ, C])
        h2T = sb("h2T", [P, KC, TT])
        xTh = sb("xTh", [P, KC, TT], F32R)
        xTl = sb("xTl", [P, KC, TT], F32R)
        wTh = sb("wTh", [P, 3, KC, C], F32R)
        wTl = sb("wTl", [P, 3, KC, C], F32R)
        woh = sb("woh", [P, KC, C], F32R)
        wol = sb("wol", [P, KC, C], F32R)
        pw = sb("pw", [P, KC, TT])
        gs = sb("gs", [P, KC, 4])
        cs = sb("cs", [P, TT + 1])
        total = sb("total", [P, KC])
        kb = sb("kb", [P, TT])
        sg = sb("sg", [P, 2, TT])
        kv = sb("kv", [P, TT])
        wk = sb("wk", [P, TT])
        aa = sb("aa", [P, 2, TT])
        sTh = sb("sTh", [P, KC, TT], F32R)
        sTl = sb("sTl", [P, KC, TT], F32R)
        h2, sidx = L["h2"], L["sidx"]
        wo_s = h2[:, 1]
        rws = sb("rws", [P, KC, GE])
        lgt = sb("lgt", [P, R * E + 2 * R])
        lg = lgt[:, 0:R * E].rearrange("p (r e) -> p r e", r=R)
        m8 = sb("m8", [P, R, 8])
        i8 = sb("i8", [P, R, 8], U32)
        ixf = sb("ixf", [P, R, 2])
        hit1 = sb("hit1", [P, R, E])
        hit2 = sb("hit2", [P, R, E])
        hits = sb("hits", [P, TJ, GE], BF16)
        qq = sb("qq", [P, TJ, GE])
        ee = sb("ee", [P, TJ, GE])
        tot = sb("tot", [P, GE])
        two = sb("two", [P, GE])
        alloc = sb("alloc", [P, 2, GE])
        incl = sb("incl", [P, GE])
        dpg = sb("dpg", [P, GE])
        used = sb("used", [P, GE])
        cur = sb("cur", [P, GE])
        fre = sb("fre", [P, G])
        slf = sb("slf", [P, 2, R])
        mod = sb("mod", [P, 5, C])
        zrow = sb("zrow", [P, 1, C])
        iota = sb("iota", [P, E])
        ones = sb("ones", [P, 1])
        tri = sb("tri", [P, P], BF16)
        oneb = sb("oneb", [P, P], BF16)
        bias = sb("bias", [P, 3, KC])
        tdc = sb("tdc", [P, KC])
        tfc = sb("tfc", [P, KC])
        gmc = sb("gmc", [P, KC])
        btc = sb("btc", [P, KC])
        half = sb("half", [P, TJ])
        stf, mvf, vaf, rsf = sb("stf", [P, TJ, 6]), sb("mvf", [P, TJ, 2]), sb("vaf", [P, TJ]), sb("rsf", [P, TJ])
        nmg = sb("nmg", [P, TJ])
        stg, mvg, vag, rsg = sb("stg", [P, TJ, 6]), sb("mvg", [P, TJ, 2]), sb("vag", [P, TJ]), sb("rsg", [P, TJ])
        stb, mvb, vab, rsb = sb("stb", [P, TJ, 6]), sb("mvb", [P, TJ, 2]), sb("vab", [P, TJ]), sb("rsb", [P, TJ])

        setup(nc, L, locals())

        x_in = [sem(f"x_in{i}") for i in range(4)]
        x1_out = sem("x1_out")
        lg_out, hist_out = sem("lg_out"), sem("hist_out")
        slots_out = [sem("slots_out0"), sem("slots_out1")]
        modf_in, modb_in, ga_in, wo_in = sem("modf_in"), sem("modb_in"), sem("ga_in"), sem("wo_in")
        cleared = [sem("cleared0"), sem("cleared1")]
        scattered = [sem("scattered0"), sem("scattered1")]
        proj_done = sem("proj_done")
        backT_done = sem("backT_done")
        logit_done = sem("logit_done")
        frontT_done = sem("frontT_done")
        out_done = sem("out_done")
        rank_done = sem("rank_done")
        k_biased = sem("k_biased")
        r_sig = sem("r_sig")
        tfkv = sem("tfkv")
        s_hi = sem("s_hi")
        h2T_copied = sem("h2T_copied")
        lg_copied = sem("lg_copied")
        x_hi = sem("x_hi")
        wo_hi = sem("wo_hi")
        z_ready = sem("z_ready")
        s_ready, s_split = sem("s_ready"), sem("s_split")
        f_rstd, g_rstd, b_rstd = sem("f_rstd"), sem("g_rstd"), sem("b_rstd")
        f_stats, f_aggr, f_var = sem("f_stats"), sem("f_aggr"), sem("f_var")
        h_half, h_ready = sem("h_half"), sem("h_ready")
        g_stats, g_aggr, g_var = sem("g_stats"), sem("g_aggr"), sem("g_var")
        g_nm = sem("g_nm")
        totaled = sem("totaled")
        x_split = sem("x_split")
        kv_ready, carry, wk_ready, scan = sem("kv_ready"), sem("carry"), sem("wk_ready"), sem("scan")
        wkv_ready = sem("wkv_ready")
        x1_ready = sem("x1_ready")
        b_stats, b_aggr, b_var = sem("b_stats"), sem("b_aggr"), sem("b_var")
        h2_half, h2_ready = sem("h2_half"), sem("h2_ready")
        top_max, top_idx = sem("top_max"), sem("top_idx")
        top_kept, idx_f, hit, hits_ready = sem("top_kept"), sem("idx_f"), sem("hit"), sem("hits_ready")
        rank_read, page_op, slot_ready = sem("rank_read"), sem("page_op"), sem("slot_ready")
        wo_scaled, wo_split = sem("wo_scaled"), sem("wo_split")
        PGOPS = 17

        def bank(s, q):
            return ps[:, (s * GROUPS + q) % NBANK, :]

        def worked(n, q):
            if n < 0:
                return n == -1 and q >= FRONTT
            behind = 2 if q == RANK else 1 if OUTP <= q < RANK or BACKT <= q < BACKT + KC or q == LOGIT else 0
            return n - behind >= 0 and n - behind < 4 * B

        def bank_free(pe, b, s, q):
            at = s * GROUPS + q - NBANK
            while isinstance(b, int) and at > -GROUPS and not worked(4 * b + at // GROUPS, at % GROUPS):
                at -= NBANK
            s0, q0 = at // GROUPS, at % GROUPS
            if q0 == LOGIT:
                who, m, v, s0 = lg_copied, 1, 1, s0 - 1
            elif BACKT <= q0 < BACKT + KC:
                who, m, v, s0 = h2T_copied, 4, q0 - BACKT + 1, s0 - 1
            elif q0 >= FRONTT:
                who, m, v, s0 = x_split, 4, q0 - FRONTT + 1, s0 + 1
            elif q0 == RANK:
                who, m, v, s0 = rank_read, 2, 2, s0 - 2
            elif OUTP <= q0 < RANK:
                who, m, v, s0 = x1_ready, 4, q0 - OUTP + 1, s0 - 1
            else:
                dc = next(i for i in range(KC) if q0 in PROJ[i])
                who, m, v = (k_biased, kv_ready, r_sig)[PROJ[dc].index(q0)], 4, dc + 1
            wait(pe, who, cnt(b, s0, m, v))

        block = ctx.enter_context(nc.Block())

        @block.sync
        def _(sp):
            def load_x(b, s):
                row = (b * (4 * TT) + s * TT) if s < 4 else ((b + 1) % B) * (4 * TT) + (s - 4) * TT
                gate(sp, (x1_out, cnt(b, s - 4, 16, 16)), (h2_half, cnt(b, s - 4, 4, 4)))
                sp.dma_start(xin[:, s % 4], xf[bass.ds(row, TT), :].rearrange("(j p) c -> p j c", p=P)
                             ).then_inc(x_in[s % 4], 16)

            def store_x1(b, s):
                wait(sp, x1_ready, cnt(b, s, 4, 4))
                row = b * (4 * TT) + s * TT
                sp.dma_start(x1_d[bass.ds(row, TT), :].rearrange("(j p) c -> p j c", p=P), xin[:, s % 4]
                             ).then_inc(x1_out, 16)

            def store_logits(b, s):
                gate(sp, (top_kept, cnt(b, s, 1, 1)))
                n = R * E + 2 * R
                sp.dma_start(lg_d[:, bass.ds(b * (4 * n) + s * n, n)], lgt[:]).then_inc(lg_out, 16)

            def store_pages(b, s):
                wait(sp, page_op, cnt(b, s, PGOPS, PGOPS))
                row = b * 4 + s
                sp.dma_start(hist_d[bass.ds(row, 1), :], incl[0:1, :]).then_inc(hist_out, 16)
                gate(sp, (slot_ready, cnt(b, s, 2, 2)))
                sp.dma_start(slots_d[:, bass.ds(b * 64 + s * 16, 16)], sidx[:, s % 2, :]).then_inc(slots_out[s % 2], 16)

            def load_mod(b, first, n, sem_):
                sp.dma_start(mod[:, first:first + n, :].rearrange("p r c -> p (r c)"),
                             mod_d[bass.ds(b, 1), first * C:(first + n) * C].to_broadcast([P, n * C])
                             ).then_inc(sem_, 16)

            zero = zrow[:]

            def fill(g, first, n):
                dst = pages[g][bass.ds(first * PAGE, n * PAGE), :].rearrange("(p r) c -> p r c", p=P)
                sp.dma_start(dst, zero.to_broadcast([P, n * PAGE // P, C])).then_inc(cleared[g], 16)

            def fills(numbers):
                for k in numbers:
                    for g in range(G):
                        wait(sp, cleared[g], 16 * k)
                        fill(g, k * FILL, FILL)

            def load_wo():
                sp.dma_start(wo_s, L["wo"].rearrange("(k p) d -> p k d", p=P)).then_inc(wo_in, 16)

            def step(b, s, first):
                if s == 0 and not first:
                    load_mod(b, GA, 1, ga_in)
                    wait(sp, scattered[1], dcnt(b, -3, 16))
                    wait(sp, backT_done, cnt(b, -3, 4, 4))
                    load_wo()
                load_x(b, s + 2)
                if not (first and s < 2):
                    store_logits(b, s - 2)
                if s == 2:
                    wait(sp, h_ready, cnt(b, 3, 4, 4))
                    load_mod((b + 1) % B, CA1, 2, modf_in)
                if not (first and s == 0):
                    store_x1(b, s - 1)
                if not (first and s < 2):
                    store_pages(b, s - 2)
                if s == 0 and not first:
                    wait(sp, h2_ready, cnt(b, -1, 4, 4))
                    load_mod(b, CB1, 2, modb_in)
                if first and s < 2:
                    fills((1, 2) if s == 0 else (3, 4))
                elif s % 2 == 0:
                    for g in range(G):
                        k = 4 + (b * 2 + s // 2)
                        wait(sp, cleared[g], (k * 16) if isinstance(k, int) else b * 32 + (4 + s // 2) * 16)
                        fill(g, k * FILL, FILL)

            load_x(0, 0)
            load_mod(0, CA1, 2, modf_in)
            load_x(0, 1)
            load_mod(0, CB1, 2, modb_in)
            load_mod(0, GA, 1, ga_in)
            load_wo()
            fills((0,))
            for s in range(4):
                step(0, s, True)
            with sp.Fori(1, B) as b:
                for s in range(4):
                    step(b, s, False)
            store_logits(B, -2)
            store_x1(B, -1)
            store_pages(B, -2)
            store_logits(B, -1)
            store_pages(B, -1)
            sp.wait_ge(x1_out, 16 * 4 * B)
            for par in range(2):
                sp.wait_ge(slots_out[par], 16 * 2 * B)
                sp.wait_ge(x_in[par], 16 * (B + 1))
                sp.wait_ge(x_in[2 + par], 16 * B)
                sp.wait_ge(cleared[par], 16 * (4 + 2 * B))
            sp.wait_ge(lg_out, 16 * 4 * B)
            sp.wait_ge(hist_out, 16 * 4 * B)
            sp.wait_ge(modf_in, 16 * (B + 1))

        @block.tensor
        def _(pe):
            def split3(o, lh, ll, rh, rl, first, last):
                nc.tensor.matmul(o, lh, rh, start=first, stop=False)
                nc.tensor.matmul(o, lh, rl, start=False, stop=False)
                return nc.tensor.matmul(o, ll, rh, start=False, stop=last)

            def project(b, s, dc, parts=(0, 1, 2)):
                d = slice(dc * P, (dc + 1) * P)
                for w in parts:
                    q = PROJ[dc][w]
                    bank_free(pe, b, s, q)
                    for k in range(KC):
                        if dc == 0 and w == 0:
                            pe.wait_ge(x_split, cnt(b, s, 4, k + 1))
                        last = split3(bank(s, q), wTh[:, w, k, d], wTl[:, w, k, d],
                                      xTh[:, k, :], xTl[:, k, :], k == 0, k == KC - 1)
                    last.then_inc(proj_done, 1)

            def back(b, s):
                pe.wait_ge(h2_ready, cnt(b, s - 1, 4, 4))
                for k in range(KC):
                    bank_free(pe, b, s, BACKT + k)
                    for j in range(TJ):
                        last = nc.tensor.transpose(bank(s, BACKT + k)[:, j * P:(j + 1) * P],
                                                   h2[:, (s - 1) % 2, j, k * P:(k + 1) * P], ident[:])
                    last.then_inc(backT_done, 1)

            def logits(b, s):
                bank_free(pe, b, s, LOGIT)
                pe.wait_ge(h2T_copied, cnt(b, s - 1, 4, 4))
                for j in range(TJ):
                    for k in range(KC):
                        last = nc.tensor.matmul(bank(s, LOGIT)[:, j * GE:(j + 1) * GE],
                                                h2T[:, k, j * P:(j + 1) * P], rws[:, k, :],
                                                start=(k == 0), stop=(k == KC - 1))
                last.then_inc(logit_done, 1)

            def front(b, s):
                pe.wait_ge(z_ready, cnt(b, s + 1, 4, 4))
                for k in range(KC):
                    bank_free(pe, b, s, FRONTT + k)
                    for j in range(TJ):
                        last = nc.tensor.transpose(bank(s, FRONTT + k)[:, j * P:(j + 1) * P],
                                                   hb[:, j, k * P:(k + 1) * P], ident[:])
                    last.then_inc(frontT_done, 1)

            def output(b, s):
                pe.wait_ge(s_split, cnt(b, s - 1, 4, 4))
                if s == 1:
                    pe.wait_ge(wo_split, b + 1)
                for j in range(TJ):
                    t = slice(j * P, (j + 1) * P)
                    bank_free(pe, b, s, OUTP + j)
                    for k in range(KC):
                        last = split3(bank(s, OUTP + j), sTh[:, k, t], sTl[:, k, t],
                                      woh[:, k, :], wol[:, k, :], k == 0, k == KC - 1)
                    last.then_inc(out_done, 1)

            def ranks(b, s):
                bank_free(pe, b, s, RANK)
                pe.wait_ge(hits_ready, cnt(b, s - 2, 1, 1))
                o = bank(s, RANK)
                for j in range(TJ):
                    for i in range(j):
                        nc.tensor.matmul(o[:, j * GE:(j + 1) * GE], oneb[:], hits[:, i, :], start=(i == 0), stop=False)
                    nc.tensor.matmul(o[:, j * GE:(j + 1) * GE], tri[:], hits[:, j, :], start=(j == 0), stop=True)
                for j in range(TJ):
                    last = nc.tensor.matmul(o[:, TJ * GE:(TJ + 1) * GE], oneb[:], hits[:, j, :],
                                            start=(j == 0), stop=(j == TJ - 1))
                last.then_inc(rank_done, 1)

            def step(b, s, first):
                project(b, s, 0)
                if not (first and s == 0):
                    output(b, s)
                if not (first and s < 2):
                    ranks(b, s)
                project(b, s, 1)
                project(b, s, 2)
                if not (first and s == 0):
                    back(b, s)
                project(b, s, 3, (0,))
                if not (first and s == 0):
                    logits(b, s)
                project(b, s, 3, (1, 2))
                front(b, s)

            front(0, -1)
            for s in range(4):
                step(0, s, True)
            with pe.Fori(1, B) as b:
                for s in range(4):
                    step(b, s, False)
            output(B, 0)
            ranks(B, 0)
            back(B, 0)
            logits(B, 0)
            ranks(B, 1)

        @block.scalar
        def _(act):
            def chunk_k(b, s, dc):
                act.wait_ge(proj_done, cnt(b, s, 12, 3 * dc + 1))
                wait(act, kv_ready, cnt(b, s, 4, dc))
                nc.scalar.activation(kb[:], bank(s, PROJ[dc][0]), ACT.Identity,
                                     bias=bias[:, 0, dc:dc + 1]).then_inc(k_biased, 1)

            def chunk_r(b, s, dc):
                act.wait_ge(proj_done, cnt(b, s, 12, 3 * dc + 3))
                wait(act, s_split, cnt(b, s, 4, dc - 1))
                nc.scalar.activation(sg[:, dc % 2, :], bank(s, PROJ[dc][2]), ACT.Sigmoid,
                                     bias=bias[:, 2, dc:dc + 1]).then_inc(r_sig, 1)

            def chunk_v(b, s, dc):
                act.wait_ge(kv_ready, cnt(b, s, 4, dc + 1))
                wait(act, s_ready, cnt(b, s, 4, dc - 1))
                nc.scalar.activation(aa[:, dc % 2, :], kv[:], ACT.Copy,
                                     scale=tfc[:, dc:dc + 1]).then_inc(tfkv, 1)

            def hi(b, s, dc):
                act.wait_ge(s_ready, cnt(b, s, 4, dc + 1))
                wait(act, out_done, cnt(b, s - 1, 4, 4))
                nc.scalar.copy(sTh[:, dc, :], sg[:, dc % 2, :]).then_inc(s_hi, 1)

            def wo(b):
                act.wait_ge(wo_scaled, b + 1)
                wait(act, out_done, cnt(b, -1, 4, 4))
                nc.scalar.copy(woh[:], wo_s).then_inc(wo_hi, 1)

            def turned(b, s):
                for k in range(KC):
                    act.wait_ge(backT_done, cnt(b, s - 1, 4, k + 1))
                    wait(act, logit_done, cnt(b, s - 2, 1, 1))
                    nc.scalar.copy(h2T[:, k, :], bank(s, BACKT + k)).then_inc(h2T_copied, 1)

            def logits(b, s):
                act.wait_ge(logit_done, cnt(b, s - 1, 1, 1))
                wait(act, lg_out, cnt(b, s - 2, 16, 16))
                wait(act, top_idx, cnt(b, s - 2, 8, 8))
                nc.scalar.copy(lgt[:, 0:R * E], bank(s, LOGIT)[:, 0:R * E]).then_inc(lg_copied, 1)

            def normed(b, s):
                act.wait_ge(g_nm, cnt(b, s + 1, 1, 1))
                for j in range(TJ):
                    nc.scalar.activation(hb[:, j, :], hb[:, j, :], ACT.Identity,
                                         bias=nmg[:, j:j + 1], scale=rsg[:, j:j + 1]).then_inc(z_ready, 1)

            def front(b, s):
                for k in range(KC):
                    act.wait_ge(frontT_done, cnt(b, s + 1, 4, k + 1))
                    wait(act, proj_done, cnt(b, s, 12, 12))
                    nc.scalar.copy(xTh[:, k, :], bank(s, FRONTT + k)).then_inc(x_hi, 1)

            def step(b, s, first):
                back_too = not (first and s == 0)
                chunk_k(b, s, 0)
                chunk_v(b, s, 0)
                chunk_r(b, s, 0)
                hi(b, s, 0)
                if s == 0:
                    wo(b)
                normed(b, s)
                chunk_k(b, s, 1)
                chunk_v(b, s, 1)
                chunk_r(b, s, 1)
                chunk_k(b, s, 2)
                if back_too:
                    turned(b, s)
                hi(b, s, 1)
                chunk_v(b, s, 2)
                chunk_r(b, s, 2)
                chunk_k(b, s, 3)
                if back_too:
                    logits(b, s)
                hi(b, s, 2)
                chunk_v(b, s, 3)
                front(b, s)
                chunk_r(b, s, 3)
                hi(b, s, 3)

            normed(0, -1)
            front(0, -1)
            for s in range(4):
                step(0, s, True)
            with act.Fori(1, B) as b:
                for s in range(4):
                    step(b, s, False)
            turned(B, 0)
            logits(B, 0)

        @block.gpsimd
        def _(pool):
            def rstd(var_sem, var, per_done, rs, done, b, s):
                pool.wait_ge(var_sem, cnt(b, s, 1, 1))
                wait(pool, per_done, cnt(b, s - 1, 4, 4))
                nc.gpsimd.tensor_tensor(rs[:], var[:], half[:], ALU.pow).then_inc(done, 1)

            def receive(b, s, dc):
                pool.wait_ge(wkv_ready, cnt(b, s, 4, dc + 1))
                pool.wait_ge(r_sig, cnt(b, s, 4, dc + 1))
                nc.gpsimd.tensor_tensor(sg[:, dc % 2, :], sg[:, dc % 2, :], aa[:, dc % 2, :], ALU.mult
                                        ).then_inc(s_ready, 1)

            def scale_wo(b):
                row = (b + 1) * 16 if isinstance(b, int) else b * 16 + 16
                pool.wait_ge(ga_in, row)
                pool.wait_ge(wo_in, row)
                nc.gpsimd.tensor_tensor(wo_s, wo_s, mod[:, GA:GA + 1, :].to_broadcast([P, KC, C]),
                                        ALU.mult).then_inc(wo_scaled, 1)

            def lo(b, s, dc):
                pool.wait_ge(s_hi, cnt(b, s, 4, dc + 1))
                wait(pool, out_done, cnt(b, s - 1, 4, 4))
                nc.gpsimd.tensor_tensor(sTl[:, dc, :], sg[:, dc % 2, :], sTh[:, dc, :].bitcast(F32),
                                        ALU.subtract).then_inc(s_split, 1)

            def scatter(b, s, first, last):
                if first == 0:
                    v = 16 * (5 + (4 * b + s) // 2) if isinstance(b, int) else b * 32 + (5 + s // 2) * 16
                    gate(pool, (slot_ready, cnt(b, s, 2, 2)), (cleared[0], v), (cleared[1], v))
                for i in range(first, last):
                    j, g = i // (2 * G), i // 2 % G
                    nc.gpsimd.indirect_dma_start(
                        out=pages[g], out_offset=bass.IndirectOffsetOnAxis(ap=sidx[:, s % 2, i:i + 1], axis=0),
                        in_=h2[:, s % 2, j, :], in_offset=None).then_inc(scattered[s % 2], 16)

            def step(b, s, first):
                old = not (first and s < 2)
                rstd(f_var, vaf, h_ready, rsf, f_rstd, b, s + 1)
                if s == 0:
                    scale_wo(b)
                receive(b, s, 0)
                lo(b, s, 0)
                rstd(g_var, vag, z_ready, rsg, g_rstd, b, s + 1)
                if not (first and s == 0):
                    rstd(b_var, vab, h2_ready, rsb, b_rstd, b, s - 1)
                if old:
                    scatter(b, s - 2, 0, 5)
                receive(b, s, 1)
                if old:
                    scatter(b, s - 2, 5, 7)
                lo(b, s, 1)
                if old:
                    scatter(b, s - 2, 7, 10)
                receive(b, s, 2)
                if old:
                    scatter(b, s - 2, 10, 12)
                lo(b, s, 2)
                if old:
                    scatter(b, s - 2, 12, 16)
                receive(b, s, 3)
                lo(b, s, 3)

            rstd(f_var, vaf, h_ready, rsf, f_rstd, 0, 0)
            rstd(g_var, vag, z_ready, rsg, g_rstd, 0, 0)
            for s in range(4):
                step(0, s, True)
            with pool.Fori(1, B) as b:
                for s in range(4):
                    step(b, s, False)
            rstd(b_var, vab, h2_ready, rsb, b_rstd, B, -1)
            scatter(B, -2, 0, 16)
            pool.wait_ge(scattered[0], 2 * B * 16 * 16)
            pool.wait_ge(scattered[1], (2 * B - 1) * 16 * 16)

        @block.vector
        def _(dve):
            V = nc.vector

            def norm_front(b, s, part):
                u = s % 4
                if part == 0:
                    dve.wait_ge(x_in[u], 16 * (b + s // 4 + 1) if isinstance(b, int) else b * 16 + (s // 4 + 1) * 16)
                    for j in range(TJ):
                        wait(dve, f_aggr, cnt(b, s - 1, 4, 4))
                        V.bn_stats(stf[:, j, :], xin[:, u, j, :]).then_inc(f_stats, 1)
                    for j in range(TJ):
                        gate(dve, (f_stats, cnt(b, s, 4, j + 1)),
                             (f_var, cnt(b, s - 1, 1, 1)), (h_half, cnt(b, s - 1, 4, 4)))
                        V.bn_aggr(mvf[:, j, :], stf[:, j, :]).then_inc(f_aggr, 1)
                    dve.wait_ge(f_aggr, cnt(b, s, 4, 4))
                    wait(dve, f_rstd, cnt(b, s - 1, 1, 1))
                    V.tensor_scalar(vaf[:], mvf[:, :, 1], EPS, None, ALU.add).then_inc(f_var, 1)
                elif part == 1:
                    if s % 4 == 0:
                        row = b + s // 4
                        dve.wait_ge(modf_in, 16 * (row + 1) if isinstance(b, int) else b * 16 + (s // 4 + 1) * 16)
                    wait(dve, frontT_done, cnt(b, s - 1, 4, 4))
                    for j in range(TJ):
                        V.scalar_tensor_tensor(out=hb[:, j, :], in0=xin[:, u, j, :], scalar=mvf[:, j, 0:1],
                                               in1=mod[:, CA1, :], op0=ALU.subtract, op1=ALU.mult).then_inc(h_half, 1)
                elif part == 2:
                    dve.wait_ge(f_rstd, cnt(b, s, 1, 1))
                    for j in range(TJ):
                        dve.wait_ge(h_half, cnt(b, s, 4, j + 1))
                        V.scalar_tensor_tensor(out=hb[:, j, :], in0=hb[:, j, :], scalar=rsf[:, j:j + 1],
                                               in1=mod[:, SA, :], op0=ALU.mult, op1=ALU.add).then_inc(h_ready, 1)
                    for j in range(TJ):
                        dve.wait_ge(h_ready, cnt(b, s, 4, j + 1))
                        wait(dve, g_aggr, cnt(b, s - 1, 4, 4))
                        V.bn_stats(stg[:, j, :], hb[:, j, :]).then_inc(g_stats, 1)
                    for j in range(TJ):
                        gate(dve, (g_stats, cnt(b, s, 4, j + 1)),
                             (g_var, cnt(b, s - 1, 1, 1)), (g_nm, cnt(b, s - 1, 1, 1)))
                        V.bn_aggr(mvg[:, j, :], stg[:, j, :]).then_inc(g_aggr, 1)
                    dve.wait_ge(g_aggr, cnt(b, s, 4, 4))
                    wait(dve, g_rstd, cnt(b, s - 1, 1, 1))
                    V.tensor_scalar(vag[:], mvg[:, :, 1], EPS, None, ALU.add).then_inc(g_var, 1)
                else:
                    dve.wait_ge(g_rstd, cnt(b, s, 1, 1))
                    wait(dve, z_ready, cnt(b, s - 1, 4, 4))
                    V.scalar_tensor_tensor(out=nmg[:], in0=mvg[:, :, 0], scalar=-1.0, in1=rsg[:],
                                           op0=ALU.mult, op1=ALU.mult).then_inc(g_nm, 1)

            def split_x(b, s):
                for k in range(KC):
                    dve.wait_ge(x_hi, cnt(b, s + 1, 4, k + 1))
                    V.tensor_tensor(xTl[:, k, :], bank(s, FRONTT + k), xTh[:, k, :].bitcast(F32),
                                    ALU.subtract).then_inc(x_split, 1)

            def chunk(b, s, dc):
                u = dc % 2
                dve.wait_ge(k_biased, cnt(b, s, 4, dc + 1))
                dve.wait_ge(proj_done, cnt(b, s, 12, 3 * dc + 2))
                wait(dve, tfkv, cnt(b, s, 4, dc))
                wait(dve, wk_ready, cnt(b, s, 4, dc))
                V.scalar_tensor_tensor(out=kv[:], in0=bank(s, PROJ[dc][1]), scalar=bias[:, 1, dc:dc + 1],
                                       in1=kb[:], op0=ALU.add, op1=ALU.mult).then_inc(kv_ready, 1)
                wait(dve, wkv_ready, cnt(b, s, 4, dc))
                wait(dve, totaled, cnt(b, s, 4, dc))
                if s == 0:
                    V.memset(cs[:, 0:1], 0.0).then_inc(carry, 1)
                else:
                    V.tensor_copy(cs[:, 0:1], total[:, dc:dc + 1]).then_inc(carry, 1)
                dve.wait_ge(kv_ready, cnt(b, s, 4, dc + 1))
                wait(dve, scan, cnt(b, s, 4, dc))
                V.scalar_tensor_tensor(out=wk[:], in0=kv[:], scalar=gs[:, dc, s:s + 1],
                                       in1=pw[:, dc, :], op0=ALU.mult, op1=ALU.mult).then_inc(wk_ready, 1)
                dve.wait_ge(wk_ready, cnt(b, s, 4, dc + 1))
                dve.wait_ge(carry, cnt(b, s, 4, dc + 1))
                V.tensor_tensor_scan(cs[:, 1:TT + 1], ones[:, 0:1].to_broadcast([P, TT]), wk[:],
                                     cs[:, 0:1], ALU.mult, ALU.add).then_inc(scan, 1)
                dve.wait_ge(scan, cnt(b, s, 4, dc + 1))
                V.tensor_copy(total[:, dc:dc + 1], cs[:, TT:TT + 1]).then_inc(totaled, 1)
                dve.wait_ge(tfkv, cnt(b, s, 4, dc + 1))
                V.scalar_tensor_tensor(out=aa[:, u, :], in0=cs[:, 0:TT], scalar=tdc[:, dc:dc + 1],
                                       in1=aa[:, u, :], op0=ALU.mult, op1=ALU.add).then_inc(wkv_ready, 1)

            def wo(b):
                dve.wait_ge(wo_hi, b + 1)
                V.tensor_tensor(wol[:], wo_s, woh[:].bitcast(F32), ALU.subtract).then_inc(wo_split, 1)

            def residual(b, s):
                u = s % 4
                for j in range(TJ):
                    dve.wait_ge(out_done, cnt(b, s, 4, j + 1))
                    V.tensor_tensor(xin[:, u, j, :], bank(s + 1, OUTP + j), xin[:, u, j, :],
                                    ALU.add).then_inc(x1_ready, 1)
                    dve.wait_ge(x1_ready, cnt(b, s, 4, j + 1))
                    wait(dve, b_aggr, cnt(b, s - 1, 4, 4))
                    V.bn_stats(stb[:, j, :], xin[:, u, j, :]).then_inc(b_stats, 1)
                for j in range(TJ):
                    gate(dve, (b_stats, cnt(b, s, 4, j + 1)),
                         (b_var, cnt(b, s - 1, 1, 1)), (h2_half, cnt(b, s - 1, 4, 4)))
                    V.bn_aggr(mvb[:, j, :], stb[:, j, :]).then_inc(b_aggr, 1)
                dve.wait_ge(b_aggr, cnt(b, s, 4, 4))
                wait(dve, b_rstd, cnt(b, s - 1, 1, 1))
                V.tensor_scalar(vab[:], mvb[:, :, 1], EPS, None, ALU.add).then_inc(b_var, 1)

            def modulate(b, s):
                u = s % 2
                if s == 0:
                    dve.wait_ge(modb_in, (b + 1) * 16 if isinstance(b, int) else b * 16 + 16)
                if s in (-1, 1):
                    dve.wait_ge(wo_split, B if isinstance(b, int) and b == B else b + 1)
                wait(dve, scattered[u], dcnt(b, s - 2, 16))
                wait(dve, backT_done, cnt(b, s - 2, 4, 4))
                for j in range(TJ):
                    V.scalar_tensor_tensor(out=h2[:, u, j, :], in0=xin[:, s % 4, j, :], scalar=mvb[:, j, 0:1],
                                           in1=mod[:, CB1, :], op0=ALU.subtract, op1=ALU.mult).then_inc(h2_half, 1)
                dve.wait_ge(b_rstd, cnt(b, s, 1, 1))
                for j in range(TJ):
                    dve.wait_ge(h2_half, cnt(b, s, 4, j + 1))
                    V.scalar_tensor_tensor(out=h2[:, u, j, :], in0=h2[:, u, j, :], scalar=rsb[:, j:j + 1],
                                           in1=mod[:, SB, :], op0=ALU.mult, op1=ALU.add).then_inc(h2_ready, 1)

            def topk(b, s):
                for r in range(R):
                    if r == 0:
                        gate(dve, (lg_copied, cnt(b, s, 1, 1)),
                             (top_idx, cnt(b, s - 1, 8, 8)), (top_kept, cnt(b, s - 1, 1, 1)))
                    V.max(m8[:, r, :], lg[:, r]).then_inc(top_max, 1)
                for r in range(R):
                    gate(dve, (top_max, cnt(b, s, 8, r + 1)), (idx_f, cnt(b, s - 1, 1, 1)))
                    V.max_index(i8[:, r, :], m8[:, r, :], lg[:, r]).then_inc(top_idx, 1)
                wait(dve, lg_out, cnt(b, s - 1, 16, 16))
                V.tensor_copy(lgt[:, R * E:].rearrange("p (r k) -> p r k", k=2), m8[:, :, 0:2]
                              ).then_inc(top_kept, 1)
                dve.wait_ge(top_idx, cnt(b, s, 8, 8))
                wait(dve, hit, cnt(b, s - 1, 2, 2))
                V.tensor_copy(ixf[:], i8[:, :, 0:2]).then_inc(idx_f, 1)
                dve.wait_ge(idx_f, cnt(b, s, 1, 1))
                wait(dve, slot_ready, cnt(b, s - 1, 2, 2))
                for k, m in enumerate((hit1, hit2)):
                    V.tensor_tensor(m[:], iota[:].unsqueeze(1).to_broadcast([P, R, E]),
                                    ixf[:, :, k:k + 1].to_broadcast([P, R, E]), ALU.is_equal).then_inc(hit, 1)
                dve.wait_ge(hit, cnt(b, s, 2, 2))
                wait(dve, rank_done, cnt(b, s - 1, 1, 1))
                V.tensor_tensor(hits[:].rearrange("p j e -> p (j e)"), hit1[:].rearrange("p r e -> p (r e)"),
                                hit2[:].rearrange("p r e -> p (r e)"), ALU.add).then_inc(hits_ready, 1)

            def place(b, s):
                n = [0]

                def op(ins):
                    n[0] += 1
                    ins.then_inc(page_op, 1)
                    return n[0]

                def after(k):
                    dve.wait_ge(page_op, cnt(b, s, PGOPS, k))

                o = bank(s + 2, RANK)
                dve.wait_ge(rank_done, cnt(b, s, 1, 1))
                wait(dve, page_op, cnt(b, s, PGOPS, 0))
                wait(dve, hist_out, cnt(b, s - 1, 16, 16))
                V.tensor_tensor(tot[:], o[:, TJ * GE:(TJ + 1) * GE], used[:], ALU.add).then_inc(rank_read, 1)
                V.tensor_tensor(qq[:], o[:, 0:TJ * GE].rearrange("p (j e) -> p j e", j=TJ),
                                used[:].unsqueeze(1).to_broadcast([P, TJ, GE]), ALU.add).then_inc(rank_read, 1)
                dve.wait_ge(rank_read, cnt(b, s, 2, 1))
                k = op(V.tensor_scalar(two[:], tot[:], 2.0 * PAGE, None, ALU.is_gt))
                after(k)
                new = op(V.scalar_tensor_tensor(out=alloc[:, 1, :], in0=tot[:], scalar=1.0 * PAGE, in1=two[:],
                                                op0=ALU.is_gt, op1=ALU.add))
                after(new)
                for g in range(G):
                    k = op(V.tensor_tensor_scan(incl[:, g * E:(g + 1) * E], ones[:, 0:1].to_broadcast([P, E]),
                                                alloc[:, 1, g * E:(g + 1) * E], fre[:, g:g + 1], ALU.mult, ALU.add))
                after(k)
                k = op(V.tensor_tensor(alloc[:, 0, :], incl[:], alloc[:, 1, :], ALU.subtract))
                kf = op(V.tensor_copy(fre[:], incl[:, E - 1:GE:E]))
                after(k)
                k = op(V.scalar_tensor_tensor(out=dpg[:], in0=alloc[:, 0, :], scalar=-1.0, in1=cur[:],
                                              op0=ALU.add, op1=ALU.subtract))
                after(k)
                dve.wait_ge(rank_read, cnt(b, s, 2, 2))
                k = op(V.scalar_tensor_tensor(out=ee[:], in0=qq[:], scalar=1.0 * PAGE,
                                              in1=dpg[:].unsqueeze(1).to_broadcast([P, TJ, GE]),
                                              op0=ALU.is_ge, op1=ALU.mult))
                after(k)
                k = op(V.tensor_tensor(ee[:], ee[:], cur[:].unsqueeze(1).to_broadcast([P, TJ, GE]), ALU.add))
                ku = op(V.scalar_tensor_tensor(out=used[:], in0=alloc[:, 1, :], scalar=-1.0 * PAGE, in1=tot[:],
                                               op0=ALU.mult, op1=ALU.add))
                kd = op(V.scalar_tensor_tensor(out=dpg[:], in0=incl[:], scalar=-1.0, in1=cur[:],
                                               op0=ALU.add, op1=ALU.subtract))
                after(k)
                k = op(V.scalar_tensor_tensor(out=ee[:], in0=ee[:], scalar=1.0 * PAGE, in1=qq[:],
                                              op0=ALU.mult, op1=ALU.add))
                after(kd)
                kd = op(V.scalar_tensor_tensor(out=dpg[:], in0=alloc[:, 1, :], scalar=0.0, in1=dpg[:],
                                               op0=ALU.is_gt, op1=ALU.mult))
                after(kd)
                kc = op(V.tensor_tensor(cur[:], cur[:], dpg[:], ALU.add))
                ev = ee[:].rearrange("p j (g e) -> p (j g) e", g=G)
                after(k)
                for i, m in enumerate((hit1, hit2)):
                    k = op(V.tensor_tensor(m[:], m[:], ev, ALU.mult))
                    if i == 0:
                        k1 = k
                assert n[0] == PGOPS - 1
                after(k1 + 1)
                wait(dve, slot_ready, cnt(b, s, 2, 0))
                k = op(V.tensor_reduce(slf[:, 0, :], hit1[:], AX_X, ALU.add))
                V.tensor_reduce(slf[:, 1, :], hit2[:], AX_X, ALU.add).then_inc(slot_ready, 1)
                after(k)
                dve.wait_ge(slot_ready, cnt(b, s, 2, 1))
                wait(dve, scattered[s % 2], dcnt(b, s - 2, 16))
                wait(dve, slots_out[s % 2], dcnt(b, s - 2))
                V.tensor_copy(sidx[:, s % 2, :].rearrange("p (r k) -> p k r", k=2), slf[:]).then_inc(slot_ready, 1)

            def step(b, s, first):
                norm_front(b, s + 1, 1)
                if not (first and s < 2):
                    topk(b, s - 2)
                chunk(b, s, 0)
                norm_front(b, s + 1, 2)
                if not (first and s == 0):
                    residual(b, s - 1)
                norm_front(b, s + 1, 3)
                if not (first and s < 2):
                    place(b, s - 2)
                if s == 0:
                    wo(b)
                if not (first and s == 0):
                    modulate(b, s - 1)
                chunk(b, s, 1)
                chunk(b, s, 2)
                norm_front(b, s + 2, 0)
                chunk(b, s, 3)
                split_x(b, s)

            for part in range(4):
                norm_front(0, 0, part)
            split_x(0, -1)
            norm_front(0, 1, 0)
            for s in range(4):
                step(0, s, True)
            with dve.Fori(1, B) as b:
                for s in range(4):
                    step(b, s, False)
            topk(B, -2)
            residual(B, -1)
            place(B, -2)
            modulate(B, -1)
            topk(B, -1)
            place(B, -1)


def setup(nc, L, A):
    B, KC, C, E, GE = L["B"], L["KC"], L["C"], L["E"], L["GE"]
    ps, ident = L["ps"], L["ident"]
    names = ("xin", "hb", "wTh", "wTl", "pw", "gs", "kb", "kv", "wk", "h2", "rws", "iota", "ones", "tri",
             "oneb", "bias", "tdc", "tfc", "gmc", "btc", "half", "used", "cur", "fre", "zrow", "aa", "sg")
    (xin, hb, wTh, wTl, pw, gs, kb, kv, wk, h2, rws, iota, ones, tri,
     oneb, bias, tdc, tfc, gmc, btc, half, used, cur, fre, zrow, aa, sg) = (A[n] for n in names)
    raw = [xin[:, i] for i in range(1, 4)]
    wm = [h2[:, 0], h2[:, 1], xin[:, 0]]
    cin = aa[:, 0, 0:KC * B].rearrange("p (k b) -> p k b", k=KC)
    csig = aa[:, 1, 0:KC * B].rearrange("p (k b) -> p k b", k=KC)
    csil = sg[:, 0, 0:KC * B].rearrange("p (k b) -> p k b", k=KC)
    tdn = sg[:, 0, KC * B:KC * B + KC]
    mrow = [hb[0:B, i, :] for i in range(KC)] + [kb[0:B, :], sg[0:B, 1, :]]
    ORDER = (SA, CA1, GA, SB, CB1, GBH)

    with ExitStack() as ctx:
        def sem(name):
            return nc.alloc_semaphore(name)

        small_in, rw_in = sem("s_small_in"), sem("s_rw_in")
        raw_in = [sem(f"s_raw_in{i}") for i in range(3)]
        wm_in = [sem(f"s_wm_in{i}") for i in range(3)]
        mod_out = sem("s_mod_out")
        filled, sel = sem("s_filled"), sem("s_sel")
        sig, biased, hi, lo, bias_kept = sem("s_sig"), sem("s_biased"), sem("s_hi_w"), sem("s_lo_w"), sem("s_bias_kept")
        silu, modded, row_done, chain = sem("s_silu"), sem("s_modded"), sem("s_row_done"), sem("s_chain")
        scaled = sem("s_scaled")
        block = ctx.enter_context(nc.Block())

        @block.sync
        def _(sp):
            for i, t in enumerate((tdc, tfc, gmc, btc)):
                sp.dma_start(t[:], L["vec"][i]).then_inc(small_in, 16)
            sp.dma_start(aa[:, 0, 0:KC * B], L["cT"]).then_inc(small_in, 16)
            for w in range(3):
                sp.dma_start(raw[w], L["wkvr"][w].rearrange("(k p) d -> p k d", p=P)).then_inc(raw_in[w], 16)
            for i in range(6):
                if i >= 3:
                    sp.wait_ge(modded, i - 2)
                sp.dma_start(wm[i % 3], L["wmod"][:, i * C:(i + 1) * C].rearrange("(k p) d -> p k d", p=P)
                             ).then_inc(wm_in[i % 3], 16)
            sp.dma_start(rws[:], L["rw"].rearrange("(k p) e -> p k e", p=P)).then_inc(rw_in, 16)
            for i, r in enumerate(ORDER):
                sp.wait_ge(row_done, i + 1)
                sp.dma_start(L["mod_d"][:, r * C:(r + 1) * C], mrow[i]).then_inc(mod_out, 16)
            sp.wait_ge(mod_out, 96)
            sp.wait_ge(rw_in, 16)

        @block.gpsimd
        def _(pool):
            g = nc.gpsimd
            g.memset(ident[:], 0.0).then_inc(filled, 1)
            g.memset(tri[:], 1.0).then_inc(filled, 1)
            g.memset(oneb[:], 1.0)
            g.memset(ones[:], 1.0)
            g.memset(half[:], -0.5)
            g.memset(zrow[:], 0.0)
            g.memset(used[:], 1.0 * PAGE)
            g.memset(cur[:], 0.0)
            g.memset(fre[:], 0.0)
            g.iota(iota[:], [[1, E]], base=0, channel_multiplier=0, allow_small_or_imprecise_dtypes=True)
            pool.wait_ge(filled, 2)
            g.affine_select(out=ident[:], in_=ident[:], compare_op=ALU.not_equal, fill=1.0, base=0,
                            pattern=[[-1, P]], channel_multiplier=1)
            g.affine_select(out=tri[:], in_=tri[:], compare_op=ALU.is_gt, fill=0.0, base=0,
                            pattern=[[1, P]], channel_multiplier=-1)

        @block.scalar
        def _(act):
            act.wait_ge(small_in, 80)
            nc.scalar.activation(tdc[:], tdc[:], ACT.Sigmoid).then_inc(sig, 1)
            nc.scalar.activation(tfc[:], tfc[:], ACT.Sigmoid).then_inc(sig, 1)
            nc.scalar.activation(csig, cin, ACT.Sigmoid).then_inc(sig, 1)
            for w in range(3):
                act.wait_ge(scaled, KC * (w + 1))
                nc.scalar.copy(wTh[:, w], raw[w]).then_inc(hi, 1)

        @block.tensor
        def _(pe):
            for w in range(3):
                pe.wait_ge(raw_in[w], 16)
                if w == 0:
                    pe.wait_ge(small_in, 80)
                for dc in range(KC):
                    for k in range(KC):
                        at = w * KC + dc
                        last = nc.tensor.matmul(ps[:, 6, at:at + 1], raw[w][:, k, dc * P:(dc + 1) * P],
                                                btc[:, k:k + 1], start=(k == 0), stop=(k == KC - 1))
                last.then_inc(biased, 1)
            pe.wait_ge(silu, 1)
            for i in range(6):
                pe.wait_ge(wm_in[i % 3], 16 * (i // 3 + 1))
                for k in range(KC):
                    last = nc.tensor.matmul(ps[0:B, i, :], csil[:, k, :], wm[i % 3][:, k, :],
                                            start=(k == 0), stop=(k == KC - 1))
                last.then_inc(modded, 1)

        @block.vector
        def _(dve):
            V = nc.vector
            n = [0]

            def link(ins):
                n[0] += 1
                ins.then_inc(chain, 1)
                dve.wait_ge(chain, n[0])

            dve.wait_ge(sig, 3)
            V.tensor_tensor(csil, cin, csig, ALU.mult).then_inc(silu, 1)
            for w in range(3):
                dve.wait_ge(raw_in[w], 16)
                dve.wait_ge(biased, w + 1)
                for k in range(KC):
                    V.tensor_scalar(raw[w][:, k, :], raw[w][:, k, :], gmc[:, k:k + 1], None,
                                    ALU.mult).then_inc(scaled, 1)
            V.tensor_copy(bias[:].rearrange("p w k -> p (w k)"), ps[:, 6, 0:3 * KC])
            for w in range(3):
                dve.wait_ge(hi, w + 1)
                V.tensor_tensor(wTl[:, w], raw[w], wTh[:, w].bitcast(F32), ALU.subtract)
            V.memset(pw[:, :, 0:1], 1.0)
            V.memset(gs[:, :, 0:1], 1.0)
            link(V.tensor_copy(tdn, tdc[:]))
            m = 1
            while m < TT:
                V.tensor_tensor(pw[:, :, m:2 * m], pw[:, :, 0:m], tdn.unsqueeze(2).to_broadcast([P, KC, m]),
                                ALU.mult).then_inc(chain, 1)
                n[0] += 1
                dve.wait_ge(chain, n[0])
                link(V.tensor_tensor(tdn, tdn, tdn, ALU.mult))
                m *= 2
            for i in range(3):
                link(V.tensor_tensor(gs[:, :, i + 1:i + 2], gs[:, :, i:i + 1], tdn.unsqueeze(2), ALU.mult))
            for i, r in enumerate(ORDER):
                dve.wait_ge(modded, i + 1)
                p = ps[0:B, i, :]
                if r in (SA, SB):
                    V.tensor_copy(mrow[i], p).then_inc(row_done, 1)
                elif r in (CA1, CB1):
                    V.tensor_scalar(mrow[i], p, 1.0, None, ALU.add).then_inc(row_done, 1)
                else:
                    sign, size = kv[0:B, :], wk[0:B, :]
                    link(V.tensor_scalar(size, p, -1.0, None, ALU.mult))
                    link(V.tensor_tensor(size, size, p, ALU.max))
                    link(V.tensor_scalar(size, size, 0.25, 0.5 if r == GBH else 1.0, ALU.max, ALU.mult))
                    link(V.tensor_scalar(sign, p, 0.0, 2.0, ALU.is_ge, ALU.mult))
                    V.scalar_tensor_tensor(out=mrow[i], in0=sign, scalar=-1.0, in1=size, op0=ALU.add,
                                           op1=ALU.mult).then_inc(row_done, 1)
                    dve.wait_ge(row_done, i + 1)


def stage_b(nc, L):
    G, E, GE, STEPS, NPG = L["G"], L["E"], L["GE"], L["STEPS"], L["NPG"]
    wts = L["wts"]
    RR = STEPS * TJ * G
    with ExitStack() as ctx:
        def sb(name, shape, dt=F32):
            return ctx.enter_context(nc.sbuf_tensor(name, shape, dt))

        def sem(name):
            return ctx.enter_context(nc.semaphore(name))

        lga = sb("b_logits", [P, STEPS, TJ * GE + 16])
        lgt = sb("b_exp", [P, RR, E])
        top2 = sb("b_top2", [P, RR])
        hist = sb("b_hist", [P, STEPS, GE])
        before = sb("b_before", [P, G, 2, STEPS, E])
        turn = sb("b_turn", [P, G, 2])
        turnu = sb("b_turnu", [P, G, 2], U32)
        pid = sb("b_page", [P, 2])
        pages_row = sb("b_pages_row", [P, 2 * P])
        own = sb("b_own", [P, G, 2])
        key = sb("b_key", [P, G, 2])
        pos = sb("b_pos", [P, G, 2])
        keys = sb("b_keys", [P, G, 2 * P])
        places = sb("b_places", [P, G, 2 * P])
        here = sb("b_here", [P, G, 2, 2 * P])
        there = sb("b_there", [P, G, 2, 2 * P])
        skey = sb("b_skey", [P, G, 2])
        slist = sb("b_slist", [P, G, 2, 2])
        slistu = sb("b_slistu", [P, G, 2, 2], U32)
        den = sb("b_den", [P, RR])
        rec = sb("b_rec", [P, RR])
        lg_in, hist_in, order_out = sem("b_lg_in"), sem("b_hist_in"), sem("b_order_out")
        scattered = sem("b_scattered")
        key_out, keys_in, pos_out, places_in = (sem(f"b_{n}") for n in ("key_out", "keys_in", "pos_out", "places_in"))
        numbered, shifted, exped, chain = sem("b_numbered"), sem("b_shifted"), sem("b_exped"), sem("b_chain")
        keyed, placed, ordered = sem("b_keyed"), sem("b_placed"), sem("b_ordered")
        lv = lga[:, :, 0:TJ * GE].rearrange("p s (r e) -> p s r e", e=E)
        tv = lga[:, :, TJ * GE:].rearrange("p s (r k) -> p s r k", k=2)
        sv = lambda t: t.rearrange("p (s r) -> p s r", s=STEPS)
        wv = wts[:].rearrange("p (r k) -> p r k", k=2)
        block = ctx.enter_context(nc.Block())

        @block.sync
        def _(sp):
            sp.dma_start(hist[:].rearrange("p s e -> p (s e)"),
                         L["hist_d"].rearrange("s e -> (s e)").unsqueeze(0).to_broadcast([P, STEPS * GE])
                         ).then_inc(hist_in, 16)
            sp.dma_start(lga[:].rearrange("p s n -> p (s n)"), L["lg_d"]).then_inc(lg_in, 16)
            for i, (done, col, out_, row, in_) in enumerate(((keyed, key, key_out, keys, keys_in),
                                                             (placed, pos, pos_out, places, places_in))):
                sp.wait_ge(done, 1)
                sp.dma_start(L["key_d"][i].rearrange("i p -> p i"), col[:].rearrange("p g c -> p (g c)"),
                             allow_slow_non_contiguous=True).then_inc(out_, 16)
                sp.wait_ge(out_, 16)
                sp.dma_start(row[:].rearrange("p g n -> p (g n)"),
                             L["key_d"][i].rearrange("i p -> (i p)").unsqueeze(0).to_broadcast([P, 2 * G * P])
                             ).then_inc(in_, 16)
            sp.wait_ge(ordered, 1)
            sp.dma_start(L["order_d"].rearrange("g k c p -> p (g k c)"), slistu[:].rearrange("p g k c -> p (g k c)"),
                         allow_slow_non_contiguous=True).then_inc(order_out, 16)
            sp.wait_ge(order_out, 16)

        @block.gpsimd
        def _(pool):
            nc.gpsimd.iota(pages_row[:], [[1, 2 * P]], base=0, channel_multiplier=0,
                           allow_small_or_imprecise_dtypes=True)
            nc.gpsimd.iota(pid[:], [[P, 2]], base=0, channel_multiplier=1,
                           allow_small_or_imprecise_dtypes=True).then_inc(numbered, 1)
            for i in range(TJ * G * 2):
                nc.gpsimd.indirect_dma_start(
                    out=L["pages"][i // 2 % G],
                    out_offset=bass.IndirectOffsetOnAxis(ap=L["sidx"][:, 1, i:i + 1], axis=0),
                    in_=L["h2"][:, 1, i // (2 * G), :], in_offset=None).then_inc(scattered, 16)
            pool.wait_ge(scattered, TJ * G * 2 * 16)

        @block.scalar
        def _(act):
            act.wait_ge(shifted, 1)
            nc.scalar.activation(lgt[:], lgt[:], ACT.Exp).then_inc(exped, 1)
            act.wait_ge(shifted, 2)
            nc.scalar.activation(top2[:], top2[:], ACT.Exp).then_inc(exped, 1)

        @block.vector
        def _(dve):
            V = nc.vector
            n = [0]

            def link(ins):
                n[0] += 1
                ins.then_inc(chain, 1)
                dve.wait_ge(chain, n[0])

            dve.wait_ge(hist_in, 16)
            dve.wait_ge(numbered, 1)
            for g in range(G):
                for c in range(2):
                    last = V.tensor_scalar(before[:, g, c], hist[:, :, g * E:(g + 1) * E], pid[:, c:c + 1], None,
                                           ALU.is_le)
            link(last)
            link(V.tensor_reduce(turn[:].rearrange("p g c -> p (g c)"),
                                 before[:].rearrange("p g c s e -> p (g c) (s e)"), AX_X, ALU.add))
            link(V.tensor_scalar(turn[:], turn[:], STEPS * E - 1.0, None, ALU.min))
            link(V.tensor_copy(turnu[:], turn[:]))
            link(V.tensor_scalar(turnu[:], turnu[:], E - 1, None, ALU.bitwise_and))
            link(V.tensor_copy(own[:], turnu[:]))
            link(V.tensor_scalar(own[:], own[:], 2.0 * P, None, ALU.mult))
            V.tensor_tensor(key[:], own[:], pid[:].unsqueeze(1).to_broadcast([P, G, 2]), ALU.add).then_inc(keyed, 1)
            dve.wait_ge(lg_in, 16)
            V.tensor_tensor(lgt[:].rearrange("p (s r) e -> p s r e", s=STEPS), lv,
                            tv[:, :, :, 0:1].to_broadcast([P, STEPS, TJ * G, E]), ALU.subtract).then_inc(shifted, 1)
            V.tensor_tensor(sv(top2[:]), tv[:, :, :, 1], tv[:, :, :, 0], ALU.subtract).then_inc(shifted, 1)
            dve.wait_ge(keyed, 1)
            dve.wait_ge(keys_in, 16)
            for g in range(G):
                for c in range(2):
                    last = V.tensor_scalar(here[:, g, c], keys[:, g], key[:, g, c:c + 1], None, ALU.is_lt)
            link(last)
            V.tensor_reduce(pos[:].rearrange("p g c -> p (g c)"), here[:].rearrange("p g c n -> p (g c) n"),
                            AX_X, ALU.add).then_inc(placed, 1)
            dve.wait_ge(exped, 1)
            link(V.tensor_reduce(den[:], lgt[:], AX_X, ALU.add))
            link(V.reciprocal(rec[:], den[:]))
            V.tensor_copy(wv[:, :, 0], rec[:])
            dve.wait_ge(exped, 2)
            V.tensor_tensor(wv[:, :, 1], rec[:], top2[:], ALU.mult)
            dve.wait_ge(placed, 1)
            dve.wait_ge(places_in, 16)
            for g in range(G):
                for c in range(2):
                    V.scalar_tensor_tensor(out=here[:, g, c], in0=places[:, g], scalar=pid[:, c:c + 1],
                                           in1=keys[:, g], op0=ALU.is_equal, op1=ALU.mult)
                    last = V.scalar_tensor_tensor(out=there[:, g, c], in0=places[:, g], scalar=pid[:, c:c + 1],
                                                  in1=pages_row[:], op0=ALU.is_equal, op1=ALU.mult)
            link(last)
            V.tensor_reduce(skey[:].rearrange("p g c -> p (g c)"), here[:].rearrange("p g c n -> p (g c) n"),
                            AX_X, ALU.add)
            for g in range(G):
                last = V.tensor_reduce(slist[:, g, 1], there[:, g], AX_X, ALU.add)
            link(last)
            link(V.tensor_tensor(skey[:], skey[:], slist[:, :, 1], ALU.subtract))
            link(V.tensor_scalar(slist[:, :, 0], skey[:], 0.5 / P, None, ALU.mult))
            V.tensor_copy(slistu[:], slist[:]).then_inc(ordered, 1)


def stage_c(nc, g, L):
    HALF = L["NPG"] // 2
    KC, C, H, NPG, NPAGES, WROW = L["KC"], L["C"], L["H"], L["NPG"], L["NPAGES"], L["WROW"]
    ps, ident, pages, order_d, wex = L["ps"], L["ident"], L["pages"][g], L["order_d"], L["wex"][g]
    J, HC = PAGE // P, H // P
    GU = KC * 2 * H
    with ExitStack() as ctx:
        def sb(name, shape, dt=F32):
            return ctx.enter_context(nc.sbuf_tensor(f"c{g}_{name}", shape, dt))

        def sem(name):
            return ctx.enter_context(nc.semaphore(f"c{g}_{name}"))

        order = sb("order", [1, 2, 2 * P], U32)
        wraw = sb("wraw", [P, 2, WROW])
        wh = sb("wh", [P, 2, WROW], F32R)
        wl = sb("wl", [P, 2, WROW], F32R)
        xp = sb("xp", [P, 2, J, C])
        xh = sb("xh", [P, 2, J, KC, P], F32R)
        xl = sb("xl", [P, 2, J, KC, P], F32R)
        sil = sb("sil", [P, J, H])
        hh = sb("hh", [P, J, H])
        hTh = sb("hTh", [P, J, HC, P], F32R)
        hTl = sb("hTl", [P, J, HC, P], F32R)
        y = sb("y", [P, 2, J, C])
        order_in = sem("order_in")
        w_in, x_in, y_out = ([sem(f"{n}{i}") for i in range(2)] for n in ("w_in", "x_in", "y_out"))
        gu_done, hT_done, xT_done, y_done = sem("gu_done"), sem("hT_done"), sem("xT_done"), sem("y_done")
        w_hi, w_lo = sem("w_hi"), sem("w_lo")
        x_hi, x_lo, silu, h_ready, h_hi, h_lo = (sem(n) for n in ("x_hi", "x_lo", "silu", "h_ready", "h_hi", "h_lo"))
        y_copied0, y_copied1 = sem("y_copied0"), sem("y_copied1")
        mixing = g == L["G"] - 1
        if mixing:
            B, slots_d, x1_d, mod_d, wts = L["B"], L["slots_d"], L["x1_d"], L["mod_d"], L["wts"]
            NT = L["N"] // P
            assert NT // 2 < HALF - 1 and NT % B == 0
            yk = sb("yk", [P, 2, 2, C])
            xr = sb("xr", [P, 2, C])
            acc = sb("acc", [P, 2, C])
            res = sb("res", [P, 2, C])
            gates = sb("gates", [P, B, C])
            si = sb("si", [P, 2, 2], U32)
            wi = sb("wi", [P, 2, 2])
            gates_in, wi_ready, first_w, second_w, gated, summed = (
                sem(n) for n in ("gates_in", "wi_ready", "first_w", "second_w", "gated", "summed"))
            si_in, rows_in, xr_in, res_out = ([sem(f"{n}{i}") for i in range(2)]
                                              for n in ("si_in", "rows_in", "xr_in", "res_out"))
        SPANS = ((1, NT // 2, True), (NT // 2, HALF - 1, False)) if mixing else ((1, HALF - 1, False),)
        PARTS = ((0, GU // 2), (GU // 2, GU), (GU, WROW))
        prow = pages.rearrange("(q j) c -> q (j c)", j=J)

        def cp(it, s, per, k):
            return it * (2 * per) + (s * per + k)

        def cd(it, s):
            return it * 16 + (s // 2 + 1) * 16

        block = ctx.enter_context(nc.Block())

        @block.sync
        def _(sp):
            def entry(k, place):
                return sp.value_load(order[0:1, k, bass.ds(place, 1)], min_val=0,
                                     max_val=(L["E"] if k == 0 else NPAGES) - 1)

            def load(it, s):
                u = s % 2
                place = it + (u * HALF + s // 2)
                gate(sp, (w_lo, cp(it, s - 2, 3, 3)))
                e = entry(0, place)

                def weights():
                    sp.dma_start(wraw[:, u, :], wex[bass.ds(e * P, P), :]).then_inc(w_in[u], 16)

                if isinstance(place, int) and place in (0, HALF):
                    weights()
                else:
                    with sp.If_ne(sp.to_reg(e), sp.to_reg(entry(0, place - 1))):
                        weights()
                    with sp.Else():
                        sp.sem_inc(w_in[u], 16)
                page = entry(1, place)
                wait(sp, xT_done, cp(it, s - 2, J, J))
                sp.dma_start(xp[:, u].rearrange("p j c -> p (j c)"), prow[bass.ds(page * P, P), :]
                             ).then_inc(x_in[u], 16)

            def store(it, s):
                page = entry(1, it + (s % 2 * HALF + s // 2))
                wait(sp, y_copied0, cp(it, s, 1, 1))
                wait(sp, y_copied1, cp(it, s, 1, 1))
                sp.dma_start(prow[bass.ds(page * P, P), :], y[:, s % 2].rearrange("p j c -> p (j c)")
                             ).then_inc(y_out[s % 2], 16)

            sp.dma_start(order[:].rearrange("o k n -> o (k n)"), order_d[g:g + 1].rearrange("g k c p -> g (k c p)")
                         ).then_inc(order_in, 16)
            sp.wait_ge(order_in, 16)
            load(0, 0)
            load(0, 1)

            def tile_in(it, s):
                u = s % 2
                t = it * 2 + s
                wait(sp, rows_in[u], it * 32)
                sp.dma_start(si[:, u], slots_d[:, bass.ds(t * (2 * L["G"]), 2)]).then_inc(si_in[u], 16)
                wait(sp, summed, cp(it, s - 2, 1, 1))
                sp.dma_start(xr[:, u], x1_d[bass.ds(t * P, P), :]).then_inc(xr_in[u], 16)

            def tile_out(it, s):
                wait(sp, summed, cp(it, s, 1, 1))
                t = it * 2 + s
                sp.dma_start(x1_d[bass.ds(t * P, P), :], res[:, s % 2]).then_inc(res_out[s % 2], 16)

            def page(it, s, first, mix):
                load(it, s + 2)
                if not (first and s == 0):
                    store(it, s - 1)
                if mix:
                    tile_in(it, s)
                    if not first:
                        tile_out(it, s - 2)

            if mixing:
                sp.dma_start(gates[:].rearrange("p b c -> p (b c)"),
                             mod_d[:, GBH * C:(GBH + 1) * C].unsqueeze(0).to_broadcast([P, B, C])
                             ).then_inc(gates_in, 16)
            for s in range(2):
                page(0, s, True, mixing)
            for a, z, mix in SPANS:
                with sp.Fori(a, z) as it:
                    for s in range(2):
                        page(it, s, False, mix)
                if mix:
                    tile_out(z, -2)
                    tile_out(z, -1)
            last = NPG // 2 - 1
            store(last, -1)
            store(last, 0)
            store(last, 1)
            for u in range(2):
                sp.wait_ge(y_out[u], 16 * (NPG // 2))
                if mixing:
                    sp.wait_ge(res_out[u], 16 * (NT // 2))

        if mixing:
            @block.gpsimd
            def _(pool):
                def gather(it, s):
                    u = s % 2
                    gate(pool, (si_in[u], cd(it, s)), (second_w, cp(it, s - 2, 1, 1)))
                    for k in range(2):
                        nc.gpsimd.indirect_dma_start(
                            out=yk[:, u, k, :], out_offset=None, in_=L["pages"][0],
                            in_offset=bass.IndirectOffsetOnAxis(ap=si[:, u, k:k + 1], axis=0)
                        ).then_inc(rows_in[u], 16)

                def finish(it, s):
                    u = s % 2
                    row = (it + s // 2) // (NT // B // 2)
                    gate(pool, (second_w, cp(it, s, 1, 1)))
                    nc.gpsimd.tensor_tensor(acc[:, u], acc[:, u],
                                            gates[:].rearrange("p b c -> p (b c)")[:, bass.ds(row * C, C)],
                                            ALU.mult).then_inc(gated, 1)
                    pool.wait_ge(gated, cp(it, s, 1, 1))
                    pool.wait_ge(xr_in[u], cd(it, s))
                    wait(pool, res_out[u], cd(it, s - 2))
                    nc.gpsimd.tensor_tensor(res[:, u], acc[:, u], xr[:, u], ALU.add).then_inc(summed, 1)

                gather(0, 0)
                gather(0, 1)
                pool.wait_ge(gates_in, 16)
                finish(0, 0)
                with pool.Fori(1, NT // 2) as it:
                    for s in range(2):
                        gather(it, s)
                        finish(it, s - 1)
                finish(NT // 2, -1)

        @block.tensor
        def _(pe):
            def split3(o, lh, ll, rh, rl, first, last):
                nc.tensor.matmul(o, lh, rh, start=first, stop=False)
                nc.tensor.matmul(o, lh, rl, start=False, stop=False)
                return nc.tensor.matmul(o, ll, rh, start=False, stop=last)

            def turn_x(it, s, j):
                if j == 0:
                    pe.wait_ge(x_in[s % 2], cd(it, s))
                wait(pe, x_lo, cp(it, s - 1, J, j + 1))
                for k in range(KC):
                    last = nc.tensor.transpose(ps[:, 4 + j, k * P:(k + 1) * P],
                                               xp[:, s % 2, j, k * P:(k + 1) * P], ident[:])
                last.then_inc(xT_done, 1)

            def gate_up(it, s, j):
                u = s % 2
                pe.wait_ge(x_lo, cp(it, s, J, j + 1))
                if j == 0:
                    pe.wait_ge(w_lo, cp(it, s, 3, 2))
                wait(pe, h_ready, cp(it, s - 1, J, j + 1))
                for k in range(KC):
                    c = slice(k * 2 * H, (k + 1) * 2 * H)
                    last = split3(ps[:, j, :], xh[:, u, j, k, :], xl[:, u, j, k, :], wh[:, u, c], wl[:, u, c],
                                  k == 0, k == KC - 1)
                last.then_inc(gu_done, 1)

            def turn_h(it, s, j):
                pe.wait_ge(h_ready, cp(it, s, J, j + 1))
                wait(pe, h_lo, cp(it, s - 1, J, j + 1))
                for q in range(HC):
                    last = nc.tensor.transpose(ps[:, 2 + j, q * P:(q + 1) * P], hh[:, j, q * P:(q + 1) * P], ident[:])
                last.then_inc(hT_done, 1)

            def down(it, s, j):
                u = s % 2
                pe.wait_ge(h_lo, cp(it, s, J, j + 1))
                if j == 0:
                    pe.wait_ge(w_lo, cp(it, s, 3, 3))
                wait(pe, (y_copied0, y_copied1)[j], cp(it, s - 1, 1, 1))
                for q in range(HC):
                    c = slice(GU + q * C, GU + (q + 1) * C)
                    last = split3(ps[:, 6 + j, :], hTh[:, j, q, :], hTl[:, j, q, :], wh[:, u, c], wl[:, u, c],
                                  q == 0, q == HC - 1)
                last.then_inc(y_done, 1)

            def page(it, s, first, final=False):
                gate_up(it, s, 0)
                if not (first and s == 0):
                    down(it, s - 1, 1)
                turn_h(it, s, 0)
                if not final:
                    turn_x(it, s + 1, 0)
                    turn_x(it, s + 1, 1)
                gate_up(it, s, 1)
                down(it, s, 0)
                turn_h(it, s, 1)

            turn_x(0, 0, 0)
            turn_x(0, 0, 1)
            for s in range(2):
                page(0, s, True)
            assert NPG % 4 == 0
            with pe.Fori(1, NPG // 2 - 1, 2) as it:
                for s in range(4):
                    page(it, s, False)
            last = NPG // 2 - 1
            page(last, 0, False)
            page(last, 1, False, True)
            down(last, 1, 1)

        @block.scalar
        def _(act):
            def whi(it, s, part):
                u, (a, z) = s % 2, PARTS[part]
                act.wait_ge(w_in[u], cd(it, s))
                if part == 2:
                    wait(act, y_done, cp(it, s - 2, J, J))
                else:
                    wait(act, gu_done, cp(it, s - 2, J, J))
                nc.scalar.copy(wh[:, u, a:z], wraw[:, u, a:z]).then_inc(w_hi, 1)

            def xhi(it, s, j):
                act.wait_ge(xT_done, cp(it, s, J, j + 1))
                wait(act, gu_done, cp(it, s - 2, J, j + 1))
                nc.scalar.copy(xh[:, s % 2, j].rearrange("p k t -> p (k t)"), ps[:, 4 + j, :]).then_inc(x_hi, 1)

            def swish(it, s, j):
                act.wait_ge(gu_done, cp(it, s, J, j + 1))
                wait(act, h_ready, cp(it, s - 1, J, j + 1))
                nc.scalar.activation(sil[:, j, :], ps[:, j, 0:H], ACT.Silu).then_inc(silu, 1)

            def hhi(it, s, j):
                act.wait_ge(hT_done, cp(it, s, J, j + 1))
                wait(act, y_done, cp(it, s - 1, J, j + 1))
                nc.scalar.copy(hTh[:, j].rearrange("p q t -> p (q t)"), ps[:, 2 + j, 0:H]).then_inc(h_hi, 1)

            def ycopy(it, s):
                act.wait_ge(y_done, cp(it, s, J, 1))
                wait(act, y_out[s % 2], cd(it, s - 2))
                nc.scalar.copy(y[:, s % 2, 0, :], ps[:, 6, :]).then_inc(y_copied0, 1)

            def weigh(it, s):
                u = s % 2
                act.wait_ge(wi_ready, cp(it, s, 1, 1))
                act.wait_ge(rows_in[u], it * 32 + (s // 2 + 1) * 32)
                wait(act, gated, cp(it, s - 2, 1, 1))
                wait(act, summed, cp(it, s - 2, 1, 1))
                nc.scalar.activation(acc[:, u], yk[:, u, 0], ACT.Copy, scale=wi[:, u, 0:1]).then_inc(first_w, 1)

            def page(it, s, final=False, mix=False):
                if not final:
                    whi(it, s + 1, 0)
                swish(it, s, 0)
                if not final:
                    whi(it, s + 1, 1)
                hhi(it, s, 0)
                if not final:
                    xhi(it, s + 1, 0)
                    xhi(it, s + 1, 1)
                    whi(it, s + 1, 2)
                swish(it, s, 1)
                if mix and not (isinstance(it, int) and s == 0):
                    weigh(it, s - 1)
                hhi(it, s, 1)
                ycopy(it, s)

            for part in range(3):
                whi(0, 0, part)
            xhi(0, 0, 0)
            xhi(0, 0, 1)
            for s in range(2):
                page(0, s, mix=mixing)
            for a, z, mix in SPANS:
                with act.Fori(a, z) as it:
                    for s in range(2):
                        page(it, s, mix=mix)
                if mix:
                    weigh(z, -1)
            last = NPG // 2 - 1
            page(last, 0)
            page(last, 1, True)

        @block.vector
        def _(dve):
            V = nc.vector

            def wlo(it, s, part):
                u, (a, z) = s % 2, PARTS[part]
                dve.wait_ge(w_hi, cp(it, s, 3, part + 1))
                V.tensor_tensor(wl[:, u, a:z], wraw[:, u, a:z], wh[:, u, a:z].bitcast(F32),
                                ALU.subtract).then_inc(w_lo, 1)

            def xlo(it, s, j):
                dve.wait_ge(x_hi, cp(it, s, J, j + 1))
                V.tensor_tensor(xl[:, s % 2, j].rearrange("p k t -> p (k t)"), ps[:, 4 + j, :],
                                xh[:, s % 2, j].rearrange("p k t -> p (k t)").bitcast(F32),
                                ALU.subtract).then_inc(x_lo, 1)

            def hidden(it, s, j):
                dve.wait_ge(silu, cp(it, s, J, j + 1))
                wait(dve, hT_done, cp(it, s - 1, J, j + 1))
                V.tensor_tensor(hh[:, j, :], ps[:, j, H:2 * H], sil[:, j, :], ALU.mult).then_inc(h_ready, 1)

            def hlo(it, s, j):
                dve.wait_ge(h_hi, cp(it, s, J, j + 1))
                V.tensor_tensor(hTl[:, j].rearrange("p q t -> p (q t)"), ps[:, 2 + j, 0:H],
                                hTh[:, j].rearrange("p q t -> p (q t)").bitcast(F32),
                                ALU.subtract).then_inc(h_lo, 1)

            def ycopy(it, s):
                dve.wait_ge(y_done, cp(it, s, J, 2))
                wait(dve, y_out[s % 2], cd(it, s - 2))
                V.tensor_copy(y[:, s % 2, 1, :], ps[:, 7, :]).then_inc(y_copied1, 1)

            def weights_for(it, s):
                wait(dve, second_w, cp(it, s - 2, 1, 1))
                gate(dve, (wi_ready, cp(it, s, 1, 0)))
                t = it * 2 + s
                V.tensor_copy(wi[:, s % 2], wts[:, bass.ds(t * (2 * L["G"]), 2)]).then_inc(wi_ready, 1)

            def weigh(it, s):
                u = s % 2
                dve.wait_ge(first_w, cp(it, s, 1, 1))
                V.scalar_tensor_tensor(out=acc[:, u], in0=yk[:, u, 1], scalar=wi[:, u, 1:2], in1=acc[:, u],
                                       op0=ALU.mult, op1=ALU.add).then_inc(second_w, 1)

            def page(it, s, first, final=False, mix=False):
                if not final:
                    wlo(it, s + 1, 0)
                hidden(it, s, 0)
                if mix:
                    weights_for(it, s)
                if not (first and s == 0):
                    ycopy(it, s - 1)
                hlo(it, s, 0)
                if not final:
                    wlo(it, s + 1, 1)
                    xlo(it, s + 1, 0)
                    xlo(it, s + 1, 1)
                    wlo(it, s + 1, 2)
                hidden(it, s, 1)
                hlo(it, s, 1)
                if mix and not (first and s == 0):
                    weigh(it, s - 1)

            for part in range(3):
                wlo(0, 0, part)
            xlo(0, 0, 0)
            xlo(0, 0, 1)
            for s in range(2):
                page(0, s, True, mix=mixing)
            for a, z, mix in SPANS:
                with dve.Fori(a, z) as it:
                    for s in range(2):
                        page(it, s, False, mix=mix)
                if mix:
                    weigh(z, -1)
            last = NPG // 2 - 1
            page(last, 0, False)
            page(last, 1, False, True)
            ycopy(last, 1)


def stage_d(nc, L):
    B, C, G, N = L["B"], L["C"], L["G"], L["N"]
    pages, x1_d, outf, mod_d, slots_d, wts = L["pages"], L["x1_d"], L["outf"], L["mod_d"], L["slots_d"], L["wts"]
    TPB = 4 * TJ
    SK = 2 * G
    K = 2
    with ExitStack() as ctx:
        def sb(name, shape, dt=F32):
            return ctx.enter_context(nc.sbuf_tensor(f"d_{name}", shape, dt))

        def sem(name):
            return ctx.enter_context(nc.semaphore(f"d_{name}"))

        NB = 4
        yk = sb("yk", [P, NB, K, C])
        xr = sb("xr", [P, NB, C])
        acc = sb("acc", [P, NB, C])
        res = sb("res", [P, NB, C])
        gb = sb("gb", [P, C])
        si = sb("si", [P, TPB * SK], U32)
        wi = sb("wi", [P, TPB * SK])
        gb_in, si_in = sem("gb_in"), sem("si_in")
        y_in, x_in, out_done = ([sem(f"{n}{i}") for i in range(NB)] for n in ("y_in", "x_in", "out_done"))
        wi_ready, first_w, second_w, gated, summed = (
            sem(n) for n in ("wi_ready", "first_w", "second_w", "gated", "summed"))

        def ct(b, t, k=1):
            return b * TPB + (t + k)

        def cb(b, t, per=1):
            return b * (TPB // NB * 16 * per) + (t // NB + 1) * (16 * per)

        block = ctx.enter_context(nc.Block())

        @block.sync
        def _(sp):
            def tile(b, t):
                wait(sp, summed, ct(b, t - NB))
                row = b * (TPB * P) + t * P
                sp.dma_start(xr[:, t % NB], x1_d[bass.ds(row, P), :]).then_inc(x_in[t % NB], 16)

            def store(b, t):
                wait(sp, summed, ct(b, t))
                row = b * (TPB * P) + t * P
                sp.dma_start(outf[bass.ds(row, P), :], res[:, t % NB]).then_inc(out_done[t % NB], 16)

            def row(b, first):
                if not first:
                    gate(sp, (gated, ct(b, -1)), *((y_in[i], cb(b, i - NB, K)) for i in range(NB)))
                sp.dma_start(si[:], slots_d[:, bass.ds(b * (TPB * SK), TPB * SK)]).then_inc(si_in, 16)
                sp.dma_start(gb[:], mod_d[bass.ds(b, 1), GBH * C:(GBH + 1) * C].to_broadcast([P, C])).then_inc(gb_in, 16)
                for t in range(TPB):
                    tile(b, t)
                    if not (first and t < 2):
                        store(b, t - 2)

            row(0, True)
            with sp.Fori(1, B) as b:
                row(b, False)
            store(B, -2)
            store(B, -1)
            for i in range(NB):
                sp.wait_ge(out_done[i], 16 * TPB // NB * B)

        @block.gpsimd
        def _(pool):
            def row(b, first):
                gate(pool, (si_in, (b + 1) * 16 if isinstance(b, int) else b * 16 + 16))
                for t in range(TPB):
                    if not (first and t < NB):
                        gate(pool, (gated, ct(b, t - NB)))
                    for k in range(K):
                        at = (t + 1) * SK - K + k
                        nc.gpsimd.indirect_dma_start(
                            out=yk[:, t % NB, k, :], out_offset=None, in_=pages[G - 1],
                            in_offset=bass.IndirectOffsetOnAxis(ap=si[:, at:at + 1], axis=0)
                        ).then_inc(y_in[t % NB], 16)

            row(0, True)
            with pool.Fori(1, B) as b:
                row(b, False)

        @block.vector
        def _(dve):
            V = nc.vector

            def row(b, first):
                n = TPB * SK
                wait(dve, gated, ct(b, -1))
                V.tensor_copy(wi[:], wts[:, bass.ds(b * n, n)]).then_inc(wi_ready, 1)
                dve.wait_ge(wi_ready, b + 1)
                dve.wait_ge(gb_in, (b + 1) * 16 if isinstance(b, int) else b * 16 + 16)
                for t in range(TPB):
                    u = t % NB
                    at = (t + 1) * SK - K
                    dve.wait_ge(y_in[u], cb(b, t, K))
                    wait(dve, summed, ct(b, t - NB))
                    V.tensor_scalar(acc[:, u], yk[:, u, 0], wi[:, at:at + 1], None, ALU.mult).then_inc(first_w, 1)
                    dve.wait_ge(first_w, ct(b, t))
                    V.scalar_tensor_tensor(out=acc[:, u], in0=yk[:, u, 1], scalar=wi[:, at + 1:at + 2],
                                           in1=acc[:, u], op0=ALU.mult, op1=ALU.add).then_inc(second_w, 1)
                    dve.wait_ge(second_w, ct(b, t))
                    V.tensor_tensor(acc[:, u], acc[:, u], gb[:], ALU.mult).then_inc(gated, 1)
                    dve.wait_ge(gated, ct(b, t))
                    dve.wait_ge(x_in[u], cb(b, t))
                    wait(dve, out_done[u], cb(b, t - NB))
                    V.tensor_tensor(res[:, u], acc[:, u], xr[:, u], ALU.add).then_inc(summed, 1)

            row(0, True)
            with dve.Fori(1, B) as b:
                row(b, False)


def kernel(**inputs):
    import numpy as np
    from concourse import bacc
    from concourse.bass_utils import run_bass_kernel_spmd

    a = {k: np.asarray(v) for k, v in inputs.items()}
    x = a["L0_attn_x"]
    E, C, H = a["L0_ffn_wg0"].shape
    KC, HC = C // P, H // P

    def experts(i):
        wg, wu = (a[f"L0_ffn_{n}{i}"].reshape(E, KC, P, H) for n in ("wg", "wu"))
        gu = np.stack([wg, wu], axis=3).transpose(0, 2, 1, 3, 4).reshape(E * P, KC * 2 * H)
        wd = a[f"L0_ffn_wd{i}"].reshape(E, HC, P, C).transpose(0, 2, 1, 3).reshape(E * P, HC * C)
        return np.concatenate([gu, wd], axis=1)

    arrays = {
        "x": x,
        "vec": np.stack([a[f"L0_attn_{n}"].reshape(KC, P).T
                         for n in ("time_decay", "time_first", "ln_gamma", "ln_beta")]),
        "wkvr": np.stack([a[f"L0_attn_W{n}"].T for n in "kvr"]),
        "wo": a["L0_attn_Wo"].T,
        "rw": np.concatenate([a["L0_ffn_router_w0"], a["L0_ffn_router_w1"]], axis=1),
        "wex0": experts(0),
        "wex1": experts(1),
        "cT": a["L0_c"].T.reshape(KC, P, -1).transpose(1, 0, 2).reshape(P, -1),
        "wmod": a["L0_wmod"],
    }
    arrays = {n: np.ascontiguousarray(v) for n, v in arrays.items()}
    nc = bacc.Bacc("TRN2", target_bir_lowering=False, num_devices=1)
    t = {n: nc.dram_tensor(n, v.shape, mybir.dt.from_np(v.dtype), kind="ExternalInput").ap()
         for n, v in arrays.items()}
    out = nc.dram_tensor("out", x.shape, mybir.dt.from_np(x.dtype), kind="ExternalOutput").ap()
    build(nc, t["x"], t["vec"], t["wkvr"], t["wo"], t["rw"],
          [t["wex0"], t["wex1"]], t["cT"], t["wmod"], out)
    r = run_bass_kernel_spmd(nc, [arrays], core_ids=[0])
    return r.results[0]["out"]
```
